# Optimizing a Trainium2 kernel written in Bass

```python
import numpy as np
import jax
import jax.numpy as jnp

def _softmax(x, axis=-1):
    return jax.nn.softmax(x, axis=axis)

def _gelu(x):
    return jax.nn.gelu(x, approximate=True)

def _silu(x):
    return jax.nn.silu(x)

def _sigmoid(x):
    return jax.nn.sigmoid(x)

def _layernorm(x, axis=-1, eps=1e-05):
    m = jnp.mean(x, axis=axis, keepdims=True)
    v = jnp.var(x, axis=axis, keepdims=True)
    return (x - m) / jnp.sqrt(v + eps)

def _scatter_add(tgt, idx, src, axis=0):
    return tgt.at[idx].add(src)

def _segment_sum(src, seg, n):
    return jax.ops.segment_sum(src, seg, n)
kernel_name = 'mk_conv_seq_d4_conv_nchw512_r2_819ffb'

def setup_inputs(seed: int=0):
    np.random.seed(seed)
    _w = jnp.asarray

    def _rec_inputs():
        import jax
        import jax.numpy as jnp
        _gk = jax.random.key(seed)
        x = -0.0003957 + 1 * jax.random.normal(jax.random.fold_in(_gk, 1), (64, 256, 14, 14), jnp.float32)
        return x
    x = _rec_inputs()

    def _L0_conv_setup():
        import jax, jax.numpy as jnp
        import numpy as np
        B, C, H, W = (64, 256, 14, 14)
        HEADS = 4
        DH = C // HEADS
        RH = RW = 7
        EPS = 1e-05
        SCALE = DH ** (-0.5)

        def _rel_pos_index():
            coords = np.stack(np.meshgrid(np.arange(RH), np.arange(RW), indexing='ij'))
            cf = coords.reshape(2, -1)
            rc = cf[:, :, None] - cf[:, None, :]
            rc = rc.transpose(1, 2, 0).copy()
            rc[:, :, 0] += RH - 1
            rc[:, :, 1] += RW - 1
            rc[:, :, 0] *= 2 * RH - 1
            return rc.sum(-1)
        REL_IDX = _rel_pos_index()

        def batchnorm(x, g, b, m, v):
            inv = g / jnp.sqrt(v + EPS)
            return x * inv[None, :, None, None] + (b - m * inv)[None, :, None, None]

        def dsconv(x, w_dw, w_pw):
            cin = x.shape[1]
            y = jax.lax.conv_general_dilated(x, w_dw, window_strides=(1, 1), padding=((1, 1), (1, 1)), dimension_numbers=('NCHW', 'OIHW', 'NCHW'), feature_group_count=cin)
            return jnp.einsum('bchw,oc->bohw', y, w_pw)

        def bilinear_to_7(x):
            hin, win = (x.shape[2], x.shape[3])
            ys = jnp.linspace(0.0, hin - 1, RH)
            xs = jnp.linspace(0.0, win - 1, RW)
            y0 = jnp.floor(ys).astype(jnp.int32)
            y1 = jnp.minimum(y0 + 1, hin - 1)
            x0 = jnp.floor(xs).astype(jnp.int32)
            x1 = jnp.minimum(x0 + 1, win - 1)
            wy = (ys - y0)[:, None]
            wx = (xs - x0)[None, :]
            v00 = x[:, :, y0][:, :, :, x0]
            v01 = x[:, :, y0][:, :, :, x1]
            v10 = x[:, :, y1][:, :, :, x0]
            v11 = x[:, :, y1][:, :, :, x1]
            top = v00 * (1 - wx) + v01 * wx
            bot = v10 * (1 - wx) + v11 * wx
            return top * (1 - wy) + bot * wy

        def _to_heads(t, h, w):
            b = t.shape[0]
            return jnp.transpose(t.reshape(b, DH, HEADS, h * w), (0, 2, 3, 1))
        key = jax.random.key(seed)
        ks = jax.random.split(key, 16)
        p = {}
        p['x'] = jax.random.normal(ks[0], (B, C, H, W), jnp.float32)
        p['bn1_g'] = jax.random.normal(ks[1], (C,), jnp.float32) * 0.1 + 1.0
        p['bn1_b'] = jax.random.normal(ks[2], (C,), jnp.float32) * 0.1
        p['bn1_m'] = jax.random.normal(ks[3], (C,), jnp.float32) * 0.1
        p['bn1_v'] = jax.random.uniform(ks[4], (C,), jnp.float32, 0.5, 1.5)
        p['w_qkv_dw'] = jax.random.normal(ks[5], (C, 1, 3, 3), jnp.float32) * 0.1
        p['w_qkv_pw'] = jax.random.normal(ks[6], (3 * C, C), jnp.float32) * C ** (-0.5)
        p['rel_table'] = jax.random.normal(ks[7], ((2 * RH - 1) * (2 * RW - 1), HEADS), jnp.float32) * 0.02
        p['w_out_dw'] = jax.random.normal(ks[8], (C, 1, 3, 3), jnp.float32) * 0.1
        p['w_out_pw'] = jax.random.normal(ks[9], (C, C), jnp.float32) * C ** (-0.5)
        p['bn2_g'] = jax.random.normal(ks[10], (C,), jnp.float32) * 0.1 + 1.0
        p['bn2_b'] = jax.random.normal(ks[11], (C,), jnp.float32) * 0.1
        p['bn2_m'] = jax.random.normal(ks[12], (C,), jnp.float32) * 0.1
        p['bn2_v'] = jax.random.uniform(ks[13], (C,), jnp.float32, 0.5, 1.5)
        p['w_mlp'] = jax.random.normal(ks[14], (C, C), jnp.float32) * C ** (-0.5)
        return p
    _L0_conv_all = _L0_conv_setup()
    _L0_conv_in = {k: v for k, v in _L0_conv_all.items() if k in ('bn1_g', 'bn1_b', 'bn1_m', 'bn1_v', 'w_qkv_dw', 'w_qkv_pw', 'rel_table', 'w_out_dw', 'w_out_pw', 'bn2_g', 'bn2_b', 'bn2_m', 'bn2_v', 'w_mlp')}
    del _L0_conv_all

    def _L1_conv_setup():
        import jax, jax.numpy as jnp
        import numpy as np
        GROUPS = 8
        EPS = 1e-05

        def group_norm(x, gamma, beta):
            B, C, H, W = x.shape
            xg = x.reshape(B, GROUPS, C // GROUPS, H, W)
            mean = xg.mean(axis=(2, 3, 4), keepdims=True)
            var = xg.var(axis=(2, 3, 4), keepdims=True)
            xg = (xg - mean) * jax.lax.rsqrt(var + EPS)
            x = xg.reshape(B, C, H, W)
            return x * gamma[None, :, None, None] + beta[None, :, None, None]
        key = jax.random.key(seed)
        ks = jax.random.split(key, 6)
        B, C, H, W = (8, 256, 32, 32)
        x = jax.random.normal(ks[0], (B, C, H, W), dtype=jnp.float32)
        gn_w = jnp.ones((C,), dtype=jnp.float32)
        gn_b = jnp.zeros((C,), dtype=jnp.float32)
        s = 1.0 / np.sqrt(C)
        qkv_w = jax.random.uniform(ks[1], (3 * C, C), minval=-s, maxval=s, dtype=jnp.float32)
        qkv_b = jax.random.uniform(ks[2], (3 * C,), minval=-s, maxval=s, dtype=jnp.float32)
        proj_w = jax.random.uniform(ks[3], (C, C), minval=-s, maxval=s, dtype=jnp.float32)
        proj_b = jax.random.uniform(ks[4], (C,), minval=-s, maxval=s, dtype=jnp.float32)
        return {'x': x, 'gn_w': gn_w, 'gn_b': gn_b, 'qkv_w': qkv_w, 'qkv_b': qkv_b, 'proj_w': proj_w, 'proj_b': proj_b}
    _L1_conv_all = _L1_conv_setup()
    _L1_conv_in = {k: v for k, v in _L1_conv_all.items() if k in ('gn_w', 'gn_b', 'qkv_w', 'qkv_b', 'proj_w', 'proj_b')}
    del _L1_conv_all

    def _L2_conv_setup():
        import jax, jax.numpy as jnp
        import numpy as np
        NUM_HEADS = 8
        NUM_GROUPS = 32
        EPS = 1e-05
        RESCALE = 1.0

        def _group_norm(x, w, b):
            B, C, L = x.shape
            g = x.reshape(B, NUM_GROUPS, C // NUM_GROUPS * L)
            mu = jnp.mean(g, axis=-1, keepdims=True)
            var = jnp.var(g, axis=-1, keepdims=True)
            g = (g - mu) * jax.lax.rsqrt(var + EPS)
            return g.reshape(B, C, L) * w[None, :, None] + b[None, :, None]
        key = jax.random.key(seed)
        ks = jax.random.split(key, 7)
        b, c, h, w = (16, 256, 32, 32)
        return {'x': jax.random.normal(ks[0], (b, c, h, w), jnp.float32), 'norm_w': jax.random.normal(ks[1], (c,), jnp.float32), 'norm_b': jax.random.normal(ks[2], (c,), jnp.float32), 'qkv_w': jax.random.normal(ks[3], (3 * c, c), jnp.float32) * c ** (-0.5), 'qkv_b': jax.random.normal(ks[4], (3 * c,), jnp.float32) * 0.02, 'proj_w': jax.random.normal(ks[5], (c, c), jnp.float32) * c ** (-0.5), 'proj_b': jax.random.normal(ks[6], (c,), jnp.float32) * 0.02}
    _L2_conv_all = _L2_conv_setup()
    _L2_conv_in = {k: v for k, v in _L2_conv_all.items() if k in ('norm_w', 'norm_b', 'qkv_w', 'qkv_b', 'proj_w', 'proj_b')}
    del _L2_conv_all

    def _L3_conv_setup():
        import jax, jax.numpy as jnp
        import numpy as np
        GROUPS = 32
        EPS = 1e-05

        def _group_norm(x, gamma, beta):
            b, c, h, w = x.shape
            xg = x.reshape(b, GROUPS, c // GROUPS, h, w)
            mean = jnp.mean(xg, axis=(2, 3, 4), keepdims=True)
            var = jnp.var(xg, axis=(2, 3, 4), keepdims=True)
            xn = ((xg - mean) * jax.lax.rsqrt(var + EPS)).reshape(b, c, h, w)
            return xn * gamma[None, :, None, None] + beta[None, :, None, None]

        def _conv1x1(x, w, bias):
            return jnp.einsum('bchw,oc->bohw', x, w) + bias[None, :, None, None]
        key = jax.random.key(seed)
        ks = jax.random.split(key, 11)
        B, C, H, W = (4, 256, 32, 32)
        s = C ** (-0.5)
        return {'x': jax.random.normal(ks[0], (B, C, H, W), dtype=jnp.float32), 'gamma': jnp.ones((C,), jnp.float32), 'beta': jnp.zeros((C,), jnp.float32), 'wq': jax.random.normal(ks[1], (C, C), jnp.float32) * s, 'bq': jnp.zeros((C,), jnp.float32), 'wk': jax.random.normal(ks[2], (C, C), jnp.float32) * s, 'bk': jnp.zeros((C,), jnp.float32), 'wv': jax.random.normal(ks[3], (C, C), jnp.float32) * s, 'bv': jnp.zeros((C,), jnp.float32), 'wo': jax.random.normal(ks[4], (C, C), jnp.float32) * s, 'bo': jnp.zeros((C,), jnp.float32)}
    _L3_conv_all = _L3_conv_setup()
    _L3_conv_in = {k: v for k, v in _L3_conv_all.items() if k in ('gamma', 'beta', 'wq', 'bq', 'wk', 'bk', 'wv', 'bv', 'wo', 'bo')}
    del _L3_conv_all
    return {'x': x, 'L0_conv_bn1_g': _L0_conv_in['bn1_g'], 'L0_conv_bn1_b': _L0_conv_in['bn1_b'], 'L0_conv_bn1_m': _L0_conv_in['bn1_m'], 'L0_conv_bn1_v': _L0_conv_in['bn1_v'], 'L0_conv_w_qkv_dw': _L0_conv_in['w_qkv_dw'], 'L0_conv_w_qkv_pw': _L0_conv_in['w_qkv_pw'], 'L0_conv_rel_table': _L0_conv_in['rel_table'], 'L0_conv_w_out_dw': _L0_conv_in['w_out_dw'], 'L0_conv_w_out_pw': _L0_conv_in['w_out_pw'], 'L0_conv_bn2_g': _L0_conv_in['bn2_g'], 'L0_conv_bn2_b': _L0_conv_in['bn2_b'], 'L0_conv_bn2_m': _L0_conv_in['bn2_m'], 'L0_conv_bn2_v': _L0_conv_in['bn2_v'], 'L0_conv_w_mlp': _L0_conv_in['w_mlp'], 'L1_conv_gn_w': _L1_conv_in['gn_w'], 'L1_conv_gn_b': _L1_conv_in['gn_b'], 'L1_conv_qkv_w': _L1_conv_in['qkv_w'], 'L1_conv_qkv_b': _L1_conv_in['qkv_b'], 'L1_conv_proj_w': _L1_conv_in['proj_w'], 'L1_conv_proj_b': _L1_conv_in['proj_b'], 'L2_conv_norm_w': _L2_conv_in['norm_w'], 'L2_conv_norm_b': _L2_conv_in['norm_b'], 'L2_conv_qkv_w': _L2_conv_in['qkv_w'], 'L2_conv_qkv_b': _L2_conv_in['qkv_b'], 'L2_conv_proj_w': _L2_conv_in['proj_w'], 'L2_conv_proj_b': _L2_conv_in['proj_b'], 'L3_conv_gamma': _L3_conv_in['gamma'], 'L3_conv_beta': _L3_conv_in['beta'], 'L3_conv_wq': _L3_conv_in['wq'], 'L3_conv_bq': _L3_conv_in['bq'], 'L3_conv_wk': _L3_conv_in['wk'], 'L3_conv_bk': _L3_conv_in['bk'], 'L3_conv_wv': _L3_conv_in['wv'], 'L3_conv_bv': _L3_conv_in['bv'], 'L3_conv_wo': _L3_conv_in['wo'], 'L3_conv_bo': _L3_conv_in['bo']}

def reference(x, L0_conv_bn1_g, L0_conv_bn1_b, L0_conv_bn1_m, L0_conv_bn1_v, L0_conv_w_qkv_dw, L0_conv_w_qkv_pw, L0_conv_rel_table, L0_conv_w_out_dw, L0_conv_w_out_pw, L0_conv_bn2_g, L0_conv_bn2_b, L0_conv_bn2_m, L0_conv_bn2_v, L0_conv_w_mlp, L1_conv_gn_w, L1_conv_gn_b, L1_conv_qkv_w, L1_conv_qkv_b, L1_conv_proj_w, L1_conv_proj_b, L2_conv_norm_w, L2_conv_norm_b, L2_conv_qkv_w, L2_conv_qkv_b, L2_conv_proj_w, L2_conv_proj_b, L3_conv_gamma, L3_conv_beta, L3_conv_wq, L3_conv_bq, L3_conv_wk, L3_conv_bk, L3_conv_wv, L3_conv_bv, L3_conv_wo, L3_conv_bo):
    import jax
    import jax.numpy as jnp

    def _L0_conv_ref(x, bn1_g, bn1_b, bn1_m, bn1_v, w_qkv_dw, w_qkv_pw, rel_table, w_out_dw, w_out_pw, bn2_g, bn2_b, bn2_m, bn2_v, w_mlp):
        import jax, jax.numpy as jnp
        import numpy as np
        B, C, H, W = (64, 256, 14, 14)
        HEADS = 4
        DH = C // HEADS
        RH = RW = 7
        EPS = 1e-05
        SCALE = DH ** (-0.5)

        def _rel_pos_index():
            coords = np.stack(np.meshgrid(np.arange(RH), np.arange(RW), indexing='ij'))
            cf = coords.reshape(2, -1)
            rc = cf[:, :, None] - cf[:, None, :]
            rc = rc.transpose(1, 2, 0).copy()
            rc[:, :, 0] += RH - 1
            rc[:, :, 1] += RW - 1
            rc[:, :, 0] *= 2 * RH - 1
            return rc.sum(-1)
        REL_IDX = _rel_pos_index()

        def batchnorm(x, g, b, m, v):
            inv = g / jnp.sqrt(v + EPS)
            return x * inv[None, :, None, None] + (b - m * inv)[None, :, None, None]

        def dsconv(x, w_dw, w_pw):
            cin = x.shape[1]
            y = jax.lax.conv_general_dilated(x, w_dw, window_strides=(1, 1), padding=((1, 1), (1, 1)), dimension_numbers=('NCHW', 'OIHW', 'NCHW'), feature_group_count=cin)
            return jnp.einsum('bchw,oc->bohw', y, w_pw)

        def bilinear_to_7(x):
            hin, win = (x.shape[2], x.shape[3])
            ys = jnp.linspace(0.0, hin - 1, RH)
            xs = jnp.linspace(0.0, win - 1, RW)
            y0 = jnp.floor(ys).astype(jnp.int32)
            y1 = jnp.minimum(y0 + 1, hin - 1)
            x0 = jnp.floor(xs).astype(jnp.int32)
            x1 = jnp.minimum(x0 + 1, win - 1)
            wy = (ys - y0)[:, None]
            wx = (xs - x0)[None, :]
            v00 = x[:, :, y0][:, :, :, x0]
            v01 = x[:, :, y0][:, :, :, x1]
            v10 = x[:, :, y1][:, :, :, x0]
            v11 = x[:, :, y1][:, :, :, x1]
            top = v00 * (1 - wx) + v01 * wx
            bot = v10 * (1 - wx) + v11 * wx
            return top * (1 - wy) + bot * wy

        def _to_heads(t, h, w):
            b = t.shape[0]
            return jnp.transpose(t.reshape(b, DH, HEADS, h * w), (0, 2, 3, 1))
        out = batchnorm(x, bn1_g, bn1_b, bn1_m, bn1_v)
        qkv = dsconv(out, w_qkv_dw, w_qkv_pw)
        q, k, v = jnp.split(qkv, 3, axis=1)
        k = bilinear_to_7(k)
        v = bilinear_to_7(v)
        q = _to_heads(q, H, W)
        k = _to_heads(k, RH, RW)
        v = _to_heads(v, RH, RW)
        attn = jnp.einsum('bhid,bhjd->bhij', q, k)
        bias = rel_table[REL_IDX.reshape(-1)].reshape(RH, RW, RH * RW, HEADS)
        bias = jnp.repeat(bias, 2, axis=0)
        bias = jnp.repeat(bias, 2, axis=1)
        bias = jnp.transpose(bias.reshape(H * W, RH * RW, HEADS), (2, 0, 1))[None]
        attn = (attn + bias) * SCALE
        attn = jax.nn.softmax(attn, axis=-1)
        o = jnp.einsum('bhij,bhjd->bhid', attn, v)
        o = jnp.transpose(o, (0, 3, 1, 2)).reshape(x.shape[0], C, H, W)
        o = dsconv(o, w_out_dw, w_out_pw)
        out = o + x
        residue = out
        out = batchnorm(out, bn2_g, bn2_b, bn2_m, bn2_v)
        out = jax.nn.relu(out)
        out = jnp.einsum('bchw,oc->bohw', out, w_mlp)
        return out + residue

    def _L1_conv_ref(x, gn_w, gn_b, qkv_w, qkv_b, proj_w, proj_b):
        import jax, jax.numpy as jnp
        import numpy as np
        GROUPS = 8
        EPS = 1e-05

        def group_norm(x, gamma, beta):
            B, C, H, W = x.shape
            xg = x.reshape(B, GROUPS, C // GROUPS, H, W)
            mean = xg.mean(axis=(2, 3, 4), keepdims=True)
            var = xg.var(axis=(2, 3, 4), keepdims=True)
            xg = (xg - mean) * jax.lax.rsqrt(var + EPS)
            x = xg.reshape(B, C, H, W)
            return x * gamma[None, :, None, None] + beta[None, :, None, None]
        B, C, H, W = x.shape
        xn = group_norm(x, gn_w, gn_b)
        xf = xn.reshape(B, C, H * W).transpose(0, 2, 1)
        qkv = jnp.einsum('bnc,dc->bnd', xf, qkv_w) + qkv_b
        q, k, v = jnp.split(qkv, 3, axis=-1)
        k = jax.nn.softmax(k, axis=-1)
        q = jax.nn.softmax(q, axis=-2)
        context = jnp.einsum('bnc,bnd->bcd', k, v)
        out = jnp.einsum('bnc,bcd->bnd', q, context)
        out = jnp.einsum('bnc,dc->bnd', out, proj_w) + proj_b
        out = out.transpose(0, 2, 1).reshape(B, C, H, W)
        return out + xn

    def _L2_conv_ref(x, norm_w, norm_b, qkv_w, qkv_b, proj_w, proj_b):
        import jax, jax.numpy as jnp
        import numpy as np
        NUM_HEADS = 8
        NUM_GROUPS = 32
        EPS = 1e-05
        RESCALE = 1.0

        def _group_norm(x, w, b):
            B, C, L = x.shape
            g = x.reshape(B, NUM_GROUPS, C // NUM_GROUPS * L)
            mu = jnp.mean(g, axis=-1, keepdims=True)
            var = jnp.var(g, axis=-1, keepdims=True)
            g = (g - mu) * jax.lax.rsqrt(var + EPS)
            return g.reshape(B, C, L) * w[None, :, None] + b[None, :, None]
        b, c, hh, ww = x.shape
        L = hh * ww
        H = NUM_HEADS
        ch = c // H
        xr = x.reshape(b, c, L)
        hid = _group_norm(xr, norm_w, norm_b)
        qkv = jnp.einsum('oc,bcl->bol', qkv_w, hid) + qkv_b[None, :, None]
        qkv = qkv.reshape(b, H, 3, ch, L)
        q, k, v = (qkv[:, :, 0], qkv[:, :, 1], qkv[:, :, 2])
        scale = 1.0 / ch ** 0.25
        weight = jnp.einsum('bhct,bhcs->bhts', q * scale, k * scale)
        weight = jax.nn.softmax(weight.astype(jnp.float32), axis=-1).astype(weight.dtype)
        a = jnp.einsum('bhts,bhcs->bhct', weight, v)
        h = a.reshape(b, c, L)
        h = jnp.einsum('oc,bcl->bol', proj_w, h) + proj_b[None, :, None]
        h = h.reshape(b, c, hh, ww)
        return (x + h) / RESCALE

    def _L3_conv_ref(x, gamma, beta, wq, bq, wk, bk, wv, bv, wo, bo):
        import jax, jax.numpy as jnp
        import numpy as np
        GROUPS = 32
        EPS = 1e-05

        def _group_norm(x, gamma, beta):
            b, c, h, w = x.shape
            xg = x.reshape(b, GROUPS, c // GROUPS, h, w)
            mean = jnp.mean(xg, axis=(2, 3, 4), keepdims=True)
            var = jnp.var(xg, axis=(2, 3, 4), keepdims=True)
            xn = ((xg - mean) * jax.lax.rsqrt(var + EPS)).reshape(b, c, h, w)
            return xn * gamma[None, :, None, None] + beta[None, :, None, None]

        def _conv1x1(x, w, bias):
            return jnp.einsum('bchw,oc->bohw', x, w) + bias[None, :, None, None]
        b, c, h, w = x.shape
        residual = x
        xn = _group_norm(x, gamma, beta)
        q = _conv1x1(xn, wq, bq).reshape(b, c, h * w)
        k = _conv1x1(xn, wk, bk).reshape(b, c, h * w)
        v = _conv1x1(xn, wv, bv).reshape(b, c, h * w)
        attn = jnp.einsum('bci,bcj->bij', q, k) * c ** (-0.5)
        attn = jax.nn.softmax(attn, axis=-1)
        out = jnp.einsum('bcj,bij->bci', v, attn).reshape(b, c, h, w)
        return residual + _conv1x1(out, wo, bo)

    def _gn(v, G=32, eps=1e-05):
        B_, C_, H_, W_ = v.shape
        g = v.reshape(B_, G, C_ // G, H_, W_)
        m = jnp.mean(g, axis=(2, 3, 4), keepdims=True)
        s = jnp.var(g, axis=(2, 3, 4), keepdims=True)
        return ((g - m) / jnp.sqrt(s + eps)).reshape(v.shape)

    def _ln_c(v, eps=1e-06):
        m = jnp.mean(v, axis=1, keepdims=True)
        s = jnp.var(v, axis=1, keepdims=True)
        return (v - m) / jnp.sqrt(s + eps)

    def _ln_t(v, eps=1e-05):
        m = jnp.mean(v, axis=-1, keepdims=True)
        s = jnp.var(v, axis=-1, keepdims=True)
        return (v - m) / jnp.sqrt(s + eps)

    def _to_tokens(v):
        B_, C_, H_, W_ = v.shape
        return v.reshape(B_, C_, H_ * W_).transpose(0, 2, 1)

    def _from_tokens(t, like):
        B_, C_, H_, W_ = like.shape
        return t.transpose(0, 2, 1).reshape(B_, C_, H_, W_)
    x = _L0_conv_ref(x, L0_conv_bn1_g, L0_conv_bn1_b, L0_conv_bn1_m, L0_conv_bn1_v, L0_conv_w_qkv_dw, L0_conv_w_qkv_pw, L0_conv_rel_table, L0_conv_w_out_dw, L0_conv_w_out_pw, L0_conv_bn2_g, L0_conv_bn2_b, L0_conv_bn2_m, L0_conv_bn2_v, L0_conv_w_mlp)
    x = _L1_conv_ref(x, L1_conv_gn_w, L1_conv_gn_b, L1_conv_qkv_w, L1_conv_qkv_b, L1_conv_proj_w, L1_conv_proj_b)
    x = _L2_conv_ref(x, L2_conv_norm_w, L2_conv_norm_b, L2_conv_qkv_w, L2_conv_qkv_b, L2_conv_proj_w, L2_conv_proj_b)
    x = _L3_conv_ref(x, L3_conv_gamma, L3_conv_beta, L3_conv_wq, L3_conv_bq, L3_conv_wk, L3_conv_bk, L3_conv_wv, L3_conv_bv, L3_conv_wo, L3_conv_bo)
    return x

_drawn_inputs = setup_inputs


def setup_inputs(seed=0):
    import zlib

    import numpy as np

    out = dict(_drawn_inputs(seed))
    spreads = {'L1_conv_gn_w': (1.0, 0.2),
     'L1_conv_gn_b': (0.0, 0.1),
     'L3_conv_gamma': (1.0, 0.2),
     'L3_conv_beta': (0.0, 0.1),
     'L3_conv_bq': (0.0, 2.0),
     'L3_conv_bk': (0.0, 2.0),
     'L3_conv_bv': (0.0, 0.1),
     'L3_conv_bo': (0.0, 0.1)}
    factors = {'L0_conv_bn1_g': 8.0,
     'L0_conv_bn1_b': 8.0,
     'L0_conv_bn1_m': 7.748,
     'L0_conv_bn1_v': 8.0,
     'L0_conv_w_qkv_dw': 4.52,
     'L0_conv_w_qkv_pw': 4.337,
     'L0_conv_rel_table': 200.0,
     'L0_conv_w_out_dw': 4.417,
     'L0_conv_w_out_pw': 4.438,
     'L2_conv_qkv_b': 4.172,
     'L2_conv_proj_b': 3.655,
     'L0_conv_bn2_b': 64.0,
     'L0_conv_bn2_m': 64.0}
    for name, (base, spread) in spreads.items():
        noise = np.random.default_rng([zlib.crc32(name.encode()), seed]).standard_normal(out[name].shape)
        drawn = base * np.exp(spread * noise) if base else spread * noise
        out[name] = jnp.asarray(drawn.astype(out[name].dtype))
    for name, factor in factors.items():
        out[name] = (out[name] * factor).astype(out[name].dtype)
    return out
```

```python
import numpy as np
import concourse.bass as bass
from concourse import mybir
from contextlib import ExitStack

F32 = mybir.dt.float32
I32 = mybir.dt.int32
ACT = mybir.ActivationFunctionType
ALU = mybir.AluOpType
AX = mybir.AxisListType

IMAGES, CH, SIDE = 64, 256, 14
TOK = SIDE * SIDE
HALF = TOK // 2
PAIRS = IMAGES // 2
KC = CH // 128
N2 = 2 * TOK
PAD = SIDE + 2
EPS = 1e-5
R7 = 7
T7 = R7 * R7
H0, D0 = 4, CH // 4
SCALE0 = D0 ** -0.5
H2, D2 = 8, CH // 8
SCALE2 = D2 ** -0.5
SCALE3 = CH ** -0.5
MAGIC = float(0x5F3759DF)
NEWTON = 3

SLOTS = 16
LOAD_X = -7
BN1 = (0, 1)
CONV1 = tuple(2 + k for k in range(9))
RESIZE = (11, 12)
L0_Q = (12, 13)
L0_K, L0_V = 14, 15
L0_S, L0_SUM = (16, 17), (17, 18)
L0_T, L0_O = (19, 20), (21, 22)
LOAD_RES = 22
CONV2 = tuple(23 + k for k in range(9))
L0_PW, L0_MLP = (32, 33), (34, 35)
GN1 = (35, 36, 37)
L1_KV, L1_Q, L1_CTX, L1_OUT = (39, 40, 41, 42), (43, 44), (45, 46), (47, 48)
GN2 = (48, 49, 50)
HOP_A, HOP_B = 54, 66
L2_QK = ((52, 53), (56, 57))
L2_V = (54, 58)
ATT = 56
UNITS = 2 * H2
L2_RDEN, L2_RT, L2_REP, L2_PROJ = ATT + UNITS, 73, (74, 75), (76, 77)
GN3 = (77, 78, 79)
L3_V, L3_Q, L3_S, L3_T, L3_O = (80, 81, 82, 83), (84, 85), (86, 87), (88, 89), (90, 91)
STORE = 91
LAST_LAG = STORE // SLOTS


W_SHAPES = {
    "bn_g": (128, 4), "bn_b": (128, 4), "bn_m": (128, 4), "bn_v": (128, 4),
    "dw1": (128, KC, 9), "frac": (128, 6),
    "q0": (128, KC, CH), "k0": (128, KC, CH), "v0": (128, KC, CH), "bias0": (HALF, 2, 4, T7),
    "dw2": (128, KC, 9), "o0": (128, KC, CH), "mlp0": (128, KC, CH),
    "gn1_w": (128, 4), "gn1_b": (128, 4), "group32": (128, 128), "group8": (128, 128),
    "q1": (128, KC, CH), "qb1": (128, KC), "kv1": (128, KC, 2 * CH), "kvb1": (HALF, 2 * CH),
    "v1": (128, KC, CH), "vb1_rep": (128, KC, HALF), "p1": (128, KC, CH), "pb1": (128, KC),
    "gn2_w": (128, 4), "gn2_b": (128, 4), "q2": (128, KC, CH), "k2": (128, KC, CH), "v2": (128, KC, CH),
    "qb2": (128, KC), "kb2": (128, KC), "vb2": (128, KC), "p2": (128, KC, CH), "pb2": (128, KC),
    "heads": (H2, KC, 128), "eye": (128, 128),
    "gn3_w": (128, 4), "gn3_b": (128, 4), "q3": (128, KC, CH), "k3": (128, KC, CH), "v3": (128, KC, CH),
    "o3": (128, KC, CH), "qb3": (128, KC), "kb3": (128, KC), "vb3": (128, KC), "ob3": (128, KC),
    "qb3_rep": (128, KC, HALF),
}
W_PARTS = {"kv1": CH, "kvb1": CH}


def build(nc, a):
    ctx = ExitStack()
    with ctx:
        def sb(name, shape, dt=F32):
            return ctx.enter_context(nc.sbuf_tensor(name, shape, dt))

        def sem(name):
            return ctx.enter_context(nc.semaphore(name))

        class Count:

            def __init__(self, name, per):
                self.sem, self.per = sem(name), per

            def at(self, p, k):
                return p * self.per + k

        class Bank:

            def __init__(self, name, tensor, uses):
                self.t = tensor
                self.before, fills, reads = {}, 0, 0
                for use, f, r in uses:
                    self.before[use] = (fills, reads, f, r)
                    fills, reads = fills + f, reads + r
                self.filled, self.emptied = Count(name + "_filled", fills), Count(name + "_emptied", reads)

            def full(self, p, use):
                fills, _, f, _ = self.before[use]
                return self.filled.at(p, fills + f)

            def free(self, p, use):
                return self.emptied.at(p, self.before[use][1])

            def read(self, p, use):
                _, reads, _, r = self.before[use]
                return self.emptied.at(p, reads + r)

        def psum(name):
            return ctx.enter_context(nc.psum_tensor(name, [128, 512], F32))

        w = {}
        for name, shape in W_SHAPES.items():
            w[name] = sb("w_" + name, list(shape))
        bn_scale, bn_shift = sb("bn_scale", [128, 4]), sb("bn_shift", [128, 4])
        bn_v, bn_half = sb("bn_v", [128, 4]), sb("bn_half", [128, 4])
        bn_y, bn_t = sb("bn_y", [128, 4]), sb("bn_t", [128, 4])
        kv1, kvb1 = w["kv1"], w["kvb1"]
        qb2s = sb("qb2s", [128, KC])
        pb2 = sb("pb2", [128, KC])
        q3 = sb("q3", [128, KC, CH])
        v3 = sb("v3", [128, KC, CH + 1])
        qu3 = sb("qu3", [128, KC])
        ob3 = sb("ob3", [128, KC])
        bqk3 = sb("bqk3", [HALF, 1])

        x_in = sb("x_in", [128, KC, N2])
        x_res = sb("x_res", [128, KC, N2])
        xpad = sb("xpad", [128, KC, 2 * PAD, PAD])
        CR = 2 * PAD - 2
        y1 = sb("y1", [128, KC, 2 * PAD, SIDE])
        rs_d = sb("rs_d", [128, 2 * SIDE, 6])
        rs_x = sb("rs_x", [128, 2 * SIDE, R7])
        rs_e = sb("rs_e", [128, 2, 6, R7])
        yr = sb("yr", [128, KC, 2, 2, 64])
        q0 = sb("q0", [128, 2, N2])
        k0 = sb("k0", [128, 2, 2, T7])
        v0 = sb("v0", [128, 2, 2, 128])
        s0 = sb("s0", [HALF, 2, 8, T7])
        m0 = sb("m0", [HALF, 2, 8])
        e0 = sb("e0", [HALF, 2, 8, T7])
        d0 = sb("d0", [HALF, 2, 8])
        r0 = sb("r0", [HALF, 2, 8])
        p0 = sb("p0", [HALF, 8, 2, 64])
        pt0 = sb("pt0", [128, 2, 2, TOK])
        opad = sb("opad", [128, 2, 2 * PAD, PAD])
        y2 = sb("y2", [128, KC, 2 * PAD, SIDE])
        res0 = sb("res0", [128, KC, N2])
        act0 = sb("act0", [128, KC, N2])
        x1 = sb("x1", [128, KC, N2])
        xn1 = sb("xn1", [128, KC, N2])
        kv = sb("kv", [HALF, 4, 2 * CH])
        nmk = sb("nmk", [HALF, 4])
        sk = sb("sk", [HALF, 4])
        rk = sb("rk", [HALF, 4])
        ke = sb("ke", [HALF, 4, CH])
        kn = sb("kn", [HALF, 4, CH])
        mq = sb("mq", [128, KC, 2])
        mqb = sb("mqb", [128, KC, 2])
        bq_less = sb("bq_less", [128, KC, 2])
        qe = sb("qe", [128, KC, N2])
        sq = sb("sq", [128, KC, 2])
        rq = sb("rq", [128, KC, 2])
        cx = sb("cx", [128, 2, KC, CH])
        x2 = sb("x2", [128, KC, N2])
        x2a = sb("x2a", [128, KC, N2])
        x2b = sb("x2b", [128, KC, N2])
        xn2 = sb("xn2", [128, KC, N2])
        q2 = sb("q2", [128, KC, N2])
        k2 = sb("k2", [128, KC, N2])
        v2 = sb("v2", [HALF, 2, 2, CH])
        nm2 = sb("nm2", [HALF, 2, 2])
        e2 = sb("e2", [HALF, 2, 2, TOK])
        den2 = sb("den2", [HALF, 4, H2])
        pt2 = sb("pt2", [HALF, 2, 2, TOK])
        araw = sb("araw", [128, 2, KC, TOK])
        rden2 = sb("rden2", [HALF, 4, H2])
        rt2 = sb("rt2", [H2, 2 * TOK])
        a2 = sb("a2", [128, 2, KC, TOK])
        x3 = sb("x3", [128, KC, N2])
        xn3 = sb("xn3", [128, KC, N2])
        v3t = sb("v3t", [HALF, 4, CH + 1])
        rb3 = sb("rb3", [HALF, 4])
        qt3 = sb("qt3", [128, KC, N2])
        m3 = sb("m3", [HALF, 4])
        t3 = sb("t3", [HALF, 4])
        u3 = sb("u3", [HALF, 4])
        nm3 = sb("nm3", [HALF, 4])
        e3 = sb("e3", [HALF, 4, TOK])
        s3 = sb("s3", [HALF, 4])
        r3 = sb("r3", [HALF, 4])
        p3 = sb("p3", [HALF, 4, TOK])
        pt3 = sb("pt3", [HALF, 2, 2, TOK])
        out = sb("out", [128, KC, N2])

        class GroupNorm:

            def __init__(self, n):
                self.stats = sb(f"gn{n}_stats", [128, 4, 6])
                self.mine = sb(f"gn{n}_mine", [128, 2, 4])
                self.sq = sb(f"gn{n}_sq", [128, 4])
                self.group = sb(f"gn{n}_group", [128, 2, 4])
                self.v = sb(f"gn{n}_v", [128, 4])
                self.half = sb(f"gn{n}_half", [128, 4])
                self.y = sb(f"gn{n}_y", [128, 4])
                self.t = sb(f"gn{n}_t", [128, 4])
                self.scale = sb(f"gn{n}_scale", [128, 4])
                self.shift = sb(f"gn{n}_shift", [128, 4])
                self.stat_steps = Count(f"gn{n}_stat_steps", 9)
                self.stats_ready = Count(f"gn{n}_stats_ready", 1)
                self.steps = Count(f"gn{n}_steps", 5 + 4 * NEWTON + 3)
                self.done = Count(f"gn{n}_done", 4)

        gn = {1: GroupNorm(1), 2: GroupNorm(2), 3: GroupNorm(3)}

        def uses(*names, reads=1):
            return [(name, 1, reads) for name in names]

        ps_b = psum("ps_b")
        bank_a = Bank("l0_attention", psum("ps_a"), [
            *uses("q0", "q1", "k"), *uses("v", reads=2), *uses("s0", "s1", "t0", "t1"), *uses("o0", "o1", reads=2)])
        bank_b = Bank("l0_tail", ps_b, uses("pw0", "pw1", "mlp0", "mlp1", "gn"))
        bank_n = Bank("l2_tail", ps_b, uses("rt", "rep0", "rep1", "proj0", "proj1", "gn"))
        bank_c = Bank("l1_main", psum("ps_c"), [
            *uses("kv0", "kv1", "kv2", "kv3"), *uses("q0", "q1", "ctx0", "ctx1", reads=2), *uses("out0", "out1")])
        bank_d = Bank("l2_head", psum("ps_d"), uses("gn", "q0", "k0", "v0", "q1", "k1", "v1"))
        bank_e = Bank("l3_main", psum("ps_e"), [
            *uses("v0", "v1", "v2", "v3", "q0", "q1"), *uses("s0", "s1", reads=2), *uses("t0", "t1"),
            *uses("o0", "o1", reads=2)])
        bank_s = Bank("l2_scores", psum("ps_s"), uses(*range(UNITS), reads=2))
        bank_t = Bank("l2_turned", psum("ps_t"), uses(*range(UNITS)))
        bank_o = Bank("l2_heads_out", psum("ps_o"), [(0, H2, 1), (1, H2, 1)])

        weights_in = sem("weights_in")
        consts_set = sem("consts_set")
        sp_held, pool_held, dve_held = sem("sp_held"), sem("pool_held"), sem("dve_held")
        bn_steps = sem("bn_steps")
        fold_filled, fold_emptied = sem("fold_filled"), sem("fold_emptied")
        x_loaded = Count("x_loaded", 16)
        res_loaded = Count("res_loaded", 16)
        bn1_done = Count("bn1_done", KC)
        conv1_steps = Count("conv1_steps", KC * 9)
        resize_steps = Count("resize_steps", KC * 9)
        l0_soft_steps = Count("l0_soft_steps", 2 * 4)
        l0_exp_done = Count("l0_exp_done", 2)
        l0_probs = Count("l0_probs", 2)
        conv2_steps = Count("conv2_steps", KC * 9)
        act0_done = Count("act0_done", KC)
        k_less = Count("k_less", 4)
        k_exp_done = Count("k_exp_done", 4)
        k_rsum = Count("k_rsum", 4)
        k_scaled = Count("k_scaled", 4)
        q_less_steps = Count("q_less_steps", KC * 3)
        q_rsum = Count("q_rsum", KC)
        hop_a_done, hop_b_done = Count("hop_a_done", 16), Count("hop_b_done", 16)
        max2_done = Count("max2_done", UNITS)
        rden_done = Count("rden_done", 1)
        l3_less_steps = Count("l3_less_steps", 2 * 5)
        l3_rsum = Count("l3_rsum", 2)
        p3_done = Count("p3_done", 4)
        stored = Count("stored", 16)
        block = ctx.enter_context(nc.Block())

        def run(eng, step):
            for t in range(-1, LAST_LAG + 1):
                step(t)
            with eng.Fori(LAST_LAG + 1, PAIRS - 1) as t:
                step(t)
            for t in range(PAIRS - 1, PAIRS + LAST_LAG):
                step(t)

        def pair_of(t, u, start):
            if start % SLOTS != u:
                return None
            p = t - start // SLOTS
            return p if not isinstance(t, int) or 0 <= p < PAIRS else None

        def linker(eng, count, p, k):
            done = [k]

            def link(ins):
                done[0] += 1
                ins.then_inc(count.sem, 1)
                eng.wait_ge(count.sem, count.at(p, done[0]))
            return link

        def has_before(p):
            return not isinstance(p, int) or p > 0

        def of_image(i):
            return slice(i * TOK, (i + 1) * TOK)

        def of_tile(i, tc):
            return slice(i * TOK + tc * HALF, i * TOK + (tc + 1) * HALF)

        def of_chunk(m):
            return slice(128 * m, 128 * (m + 1))

        def conv_images(tile, c):
            return tile[:, c].rearrange("p (i r) n -> p i r n", i=2)[:, :, 0:SIDE, :]

        def inside(tile, c):
            return tile[:, c].rearrange("p (i r) n -> p i r n", i=2)[:, :, 1:SIDE + 1, 1:SIDE + 1]

        def window(tile, c, k):
            return tile[:, c, k // 3:k // 3 + CR, k % 3:k % 3 + SIDE]

        def turned(n):
            return pt2[:, n % 2].rearrange("p c n -> p (c n)")

        WEIGHTS = 16 * len(W_SHAPES)
        CONSTS = 5
        BN_STEPS = 3 + 3 * NEWTON + 3 + 1
        FOLDS = 6
        FOLD_COPIES = 11

        @block.sync
        def _(sp):
            for name in W_SHAPES:
                dst = w[name][:]
                if name in W_PARTS:
                    dst = dst[..., 0:W_PARTS[name]]
                sp.dma_start(dst, a[name]).then_inc(weights_in, 16)
            sp.wait_ge(weights_in, WEIGHTS)

            def alone():
                sp.sem_inc(sp_held, 1)

            def step(t):
                for u in range(SLOTS):
                    p = pair_of(t, u, LOAD_X)
                    if p is not None:
                        sp.wait_ge(bn1_done.sem, bn1_done.at(p, 0))
                        alone()
                        sp.dma_start(x_in[:].rearrange("p c n -> p (c n)"),
                                     a["x"][bass.ds(p, 1)].rearrange("o p n -> (o p) n")).then_inc(x_loaded.sem, 16)
                    p = pair_of(t, u, LOAD_RES)
                    if p is not None:
                        sp.wait_ge(bank_b.emptied.sem, bank_b.free(p, "pw0"))
                        alone()
                        sp.dma_start(x_res[:].rearrange("p c n -> p (c n)"),
                                     a["x"][bass.ds(p, 1)].rearrange("o p n -> (o p) n")).then_inc(res_loaded.sem, 16)
                    p = pair_of(t, u, HOP_A)
                    if p is not None:
                        sp.wait_ge(bank_c.emptied.sem, bank_c.read(p, "out1"))
                        alone()
                        sp.wait_ge(hop_b_done.sem, hop_b_done.at(p, 0))
                        alone()
                        sp.dma_start(x2a[:], x2[:]).then_inc(hop_a_done.sem, 16)
                    p = pair_of(t, u, HOP_B)
                    if p is not None:
                        sp.wait_ge(hop_a_done.sem, hop_a_done.at(p, 16))
                        alone()
                        sp.wait_ge(bank_n.emptied.sem, bank_n.free(p, "rt"))
                        alone()
                        sp.dma_start(x2b[:], x2a[:]).then_inc(hop_b_done.sem, 16)
                    p = pair_of(t, u, STORE)
                    if p is not None:
                        sp.wait_ge(bank_e.emptied.sem, bank_e.read(p, "o1"))
                        alone()
                        sp.dma_start(a["out"][bass.ds(p, 1)].rearrange("o p n -> (o p) n"),
                                     out[:].rearrange("p c n -> p (c n)")).then_inc(stored.sem, 16)
            run(sp, step)
            sp.wait_ge(stored.sem, stored.at(PAIRS, 0))

        @block.gpsimd
        def _(pool):
            g = nc.gpsimd
            for tile in (xpad, opad, yr, p0, v0):
                g.memset(tile[:], 0.0).then_inc(consts_set, 1)
            pool.wait_ge(consts_set, CONSTS)
            pool.wait_ge(weights_in, WEIGHTS)

            def alone():
                pool.sem_inc(pool_held, 1)

            def resize(p, c):
                link = linker(pool, resize_steps, p, 9 * c)
                pool.wait_ge(conv1_steps.sem, conv1_steps.at(p, KC * 8 + c + 1))
                y = conv_images(y1, c)
                d = rs_d[:].rearrange("p (i r) n -> p i r n", i=2)
                x = rs_x[:].rearrange("p (i r) n -> p i r n", i=2)
                frac_x = w["frac"][:].unsqueeze(1).broadcast_to([128, 2 * SIDE, 6])
                frac_y = w["frac"][:].unsqueeze(1).unsqueeze(3).broadcast_to([128, 2, 6, R7])
                link(g.tensor_tensor(d, y[:, :, :, 1:12:2], y[:, :, :, 0:11:2], ALU.subtract))
                link(g.tensor_tensor(rs_d[:], rs_d[:], frac_x, ALU.mult))
                link(g.tensor_tensor(x[:, :, :, 0:6], y[:, :, :, 0:11:2], d, ALU.add))
                alone()
                link(g.tensor_copy(x[:, :, :, 6], y[:, :, :, 13]))
                link(g.tensor_tensor(rs_e[:], x[:, :, 1:12:2, :], x[:, :, 0:11:2, :], ALU.subtract))
                link(g.tensor_tensor(rs_e[:], rs_e[:], frac_y, ALU.mult))
                if has_before(p):
                    pool.wait_ge(bank_a.emptied.sem, bank_a.read(p - 1, "v"))
                first = yr[:, c, :, 0, 0:T7].rearrange("p i (a b) -> p i a b", a=R7)
                link(g.tensor_tensor(first[:, :, 0:6, :], x[:, :, 0:11:2, :], rs_e[:], ALU.add))
                alone()
                link(g.tensor_copy(first[:, :, 6, :], x[:, :, 13, :]))
                alone()
                link(g.tensor_copy(yr[:, c, :, 1, 0:T7], yr[:, c, :, 0, 0:T7]))

            def normalized(p, n, bank, src, dst):
                t = gn[n]
                weight, bias = w[f"gn{n}_w"], w[f"gn{n}_b"]
                link = linker(pool, t.steps, p, 0)
                pool.wait_ge(bank.emptied.sem, bank.read(p, "gn"))
                pool.wait_ge(t.done.sem, t.done.at(p, 0))
                link(g.tensor_tensor(t.t[:], t.group[:, 0], t.group[:, 0], ALU.mult))
                link(g.tensor_tensor(t.v[:], t.group[:, 1], t.t[:], ALU.subtract))
                alone()
                link(g.tensor_scalar(t.v[:], t.v[:], 0.0, EPS, ALU.max, ALU.add))
                alone()
                link(g.tensor_scalar(t.half[:], t.v[:], -0.5, None, ALU.mult))
                alone()
                link(g.tensor_scalar(t.y[:].bitcast(I32), t.v[:].bitcast(I32), -0.5, MAGIC, ALU.mult, ALU.add))
                for _ in range(NEWTON):
                    link(g.tensor_tensor(t.t[:], t.y[:], t.y[:], ALU.mult))
                    link(g.tensor_tensor(t.t[:], t.t[:], t.half[:], ALU.mult))
                    alone()
                    link(g.tensor_scalar(t.t[:], t.t[:], 1.5, None, ALU.add))
                    link(g.tensor_tensor(t.y[:], t.y[:], t.t[:], ALU.mult))
                link(g.tensor_tensor(t.scale[:], t.y[:], weight[:], ALU.mult))
                link(g.tensor_tensor(t.t[:], t.group[:, 0], t.scale[:], ALU.mult))
                link(g.tensor_tensor(t.shift[:], bias[:], t.t[:], ALU.subtract))
                for c in range(KC):
                    for i in range(2):
                        j = 2 * c + i
                        alone()
                        g.tensor_scalar(dst[:, c, of_image(i)], src[:, c, of_image(i)], t.scale[:, j:j + 1],
                                        t.shift[:, j:j + 1], ALU.mult, ALU.add).then_inc(t.done.sem, 1)

            def step(t):
                for u in range(SLOTS):
                    for i in range(2):
                        p = pair_of(t, u, L0_SUM[i])
                        if p is not None:
                            pool.wait_ge(l0_soft_steps.sem, l0_soft_steps.at(p, 4 * (i + 1)))
                            pool.wait_ge(bank_a.emptied.sem, bank_a.free(p, "q0"))
                            g.tensor_tensor(p0[:, :, i, 0:T7], e0[:, i], r0[:, i].unsqueeze(2).broadcast_to([HALF, 8, T7]),
                                            ALU.mult).then_inc(l0_probs.sem, 1)
                    for j in range(4):
                        p = pair_of(t, u, L1_KV[j] + 1)
                        if p is not None:
                            pool.wait_ge(k_rsum.sem, k_rsum.at(p, j + 1))
                            pool.wait_ge(bank_c.emptied.sem, bank_c.free(p, "kv0"))
                            alone()
                            g.tensor_scalar(kn[:, j], ke[:, j], rk[:, j:j + 1], None, ALU.mult).then_inc(k_scaled.sem, 1)
                    for i in range(2):
                        p = pair_of(t, u, L3_S[i] + 1)
                        if p is not None:
                            pool.wait_ge(l3_rsum.sem, l3_rsum.at(p, i + 1))
                            pool.wait_ge(bank_e.emptied.sem, bank_e.free(p, "v0"))
                            for tc in range(2):
                                j = 2 * i + tc
                                alone()
                                g.tensor_scalar(p3[:, j], e3[:, j], r3[:, j:j + 1], None, ALU.mult).then_inc(p3_done.sem, 1)
                    p = pair_of(t, u, GN1[2])
                    if p is not None:
                        pool.wait_ge(bank_c.emptied.sem, bank_c.free(p, "kv0"))
                        normalized(p, 1, bank_b, x1, xn1)
                    p = pair_of(t, u, GN2[2])
                    if p is not None:
                        pool.wait_ge(bank_d.emptied.sem, bank_d.free(p, "gn"))
                        normalized(p, 2, bank_d, x2, xn2)
                    p = pair_of(t, u, GN3[2])
                    if p is not None:
                        pool.wait_ge(bank_e.emptied.sem, bank_e.free(p, "v0"))
                        normalized(p, 3, bank_n, x3, xn3)
                    for c in range(KC):
                        p = pair_of(t, u, RESIZE[c])
                        if p is not None:
                            resize(p, c)
            run(pool, step)

        @block.scalar
        def _(act):
            s = nc.scalar
            act.wait_ge(weights_in, WEIGHTS)
            act.wait_ge(bn_steps, BN_STEPS)
            act.wait_ge(consts_set, CONSTS)
            act.wait_ge(fold_emptied, FOLD_COPIES)

            def step(t):
                for u in range(SLOTS):
                    for n in range(1, UNITS, 2):
                        p = pair_of(t, u, ATT + n + 1)
                        if p is not None:
                            act.wait_ge(bank_t.filled.sem, bank_t.full(p, n))
                            act.wait_ge(bank_o.filled.sem, bank_o.filled.at(p, max(n - 1, 0)))
                            s.copy(turned(n), bank_t.t[0:HALF, 0:N2]).then_inc(bank_t.emptied.sem, 1)
                    for n in range(UNITS):
                        p = pair_of(t, u, ATT + n)
                        if p is not None:
                            i, h = n // H2, n % H2
                            act.wait_ge(max2_done.sem, max2_done.at(p, n + 1))
                            if n or has_before(p):
                                act.wait_ge(bank_t.filled.sem, bank_t.filled.at(p, n - 1))
                            if h == 0:
                                act.wait_ge(rden_done.sem, rden_done.at(p, 0))
                            for tc in range(2):
                                s.activation(e2[:, n % 2, tc], bank_s.t[0:HALF, of_image(tc)], ACT.Exp,
                                             bias=nm2[:, n % 2, tc:tc + 1], accum_out=den2[:, 2 * i + tc, h:h + 1]
                                             ).then_inc(bank_s.emptied.sem, 1)
                    for i in range(2):
                        p = pair_of(t, u, ATT + H2 * (i + 1) + 1)
                        if p is not None:
                            act.wait_ge(bank_o.filled.sem, bank_o.full(p, i))
                            act.wait_ge(bank_n.emptied.sem, bank_n.free(p, "rt"))
                            s.copy(araw[:, i].rearrange("p c n -> p (c n)"), bank_o.t[:, 0:N2]).then_inc(bank_o.emptied.sem, 1)
                    for c in range(KC):
                        p = pair_of(t, u, BN1[c])
                        if p is not None:
                            act.wait_ge(x_loaded.sem, x_loaded.at(p, 16))
                            if has_before(p):
                                act.wait_ge(conv1_steps.sem, conv1_steps.at(p - 1, KC * 8 + c + 1))
                            s.activation(inside(xpad, c), x_in[:, c].rearrange("p (i r n) -> p i r n", i=2, r=SIDE),
                                         ACT.Identity, scale=bn_scale[:, c:c + 1], bias=bn_shift[:, c:c + 1]
                                         ).then_inc(bn1_done.sem, 1)
                    for c in range(KC):
                        p = pair_of(t, u, L0_Q[c])
                        if p is not None:
                            act.wait_ge(bank_a.filled.sem, bank_a.full(p, f"q{c}"))
                            s.copy(q0[:, c], bank_a.t[:, 0:N2]).then_inc(bank_a.emptied.sem, 1)
                    p = pair_of(t, u, L0_K)
                    if p is not None:
                        act.wait_ge(bank_a.filled.sem, bank_a.full(p, "k"))
                        s.copy(k0[:].rearrange("p m i n -> p (m i n)"), bank_a.t[:, 0:4 * T7]).then_inc(bank_a.emptied.sem, 1)
                    p = pair_of(t, u, L0_V)
                    if p is not None:
                        act.wait_ge(bank_a.filled.sem, bank_a.full(p, "v"))
                        src = bank_a.t[:].rearrange("p (i m d) -> p i m d", i=2, m=2)
                        for hl in range(2):
                            half = slice(64 * hl, 64 * hl + 64)
                            s.copy(v0[half, :, :, half], src[half, :, :, half]).then_inc(bank_a.emptied.sem, 1)
                    for i in range(2):
                        p = pair_of(t, u, L0_S[i])
                        if p is not None:
                            act.wait_ge(l0_soft_steps.sem, l0_soft_steps.at(p, 4 * i + 2))
                            act.wait_ge(l0_probs.sem, l0_probs.at(p, 0))
                            s.activation(e0[:, i], s0[:, i], ACT.Exp, scale=SCALE0).then_inc(l0_exp_done.sem, 1)
                        p = pair_of(t, u, L0_T[i])
                        if p is not None:
                            act.wait_ge(bank_a.filled.sem, bank_a.full(p, f"t{i}"))
                            s.copy(pt0[:, i].rearrange("p m n -> p (m n)"), bank_a.t[:, 0:N2]).then_inc(bank_a.emptied.sem, 1)
                        p = pair_of(t, u, L0_O[i])
                        if p is not None:
                            act.wait_ge(bank_a.filled.sem, bank_a.full(p, f"o{i}"))
                            act.wait_ge(conv2_steps.sem, conv2_steps.at(p, 0))
                            for m in range(2):
                                s.copy(opad[:, m, i * PAD + 1:i * PAD + 1 + SIDE, 1:SIDE + 1],
                                       bank_a.t[:, of_image(m)].rearrange("p (r n) -> p r n", r=SIDE)
                                       ).then_inc(bank_a.emptied.sem, 1)
                    for c in range(KC):
                        p = pair_of(t, u, L0_PW[c])
                        if p is not None:
                            act.wait_ge(bank_b.emptied.sem, bank_b.read(p, f"pw{c}"))
                            s.activation(act0[:, c], res0[:, c], ACT.Relu, scale=bn_scale[:, 2 + c:3 + c],
                                         bias=bn_shift[:, 2 + c:3 + c]).then_inc(act0_done.sem, 1)
                    for j in range(4):
                        p = pair_of(t, u, L1_KV[j])
                        if p is not None:
                            act.wait_ge(k_less.sem, k_less.at(p, j + 1))
                            act.wait_ge(k_scaled.sem, k_scaled.at(p, 0))
                            s.activation(ke[:, j], kv[:, j, 0:CH], ACT.Exp, bias=nmk[:, j:j + 1],
                                         accum_out=sk[:, j:j + 1]).then_inc(k_exp_done.sem, 1)
                    for c in range(KC):
                        p = pair_of(t, u, L1_Q[c])
                        if p is not None:
                            act.wait_ge(q_less_steps.sem, q_less_steps.at(p, 3 * (c + 1)))
                            for i in range(2):
                                s.activation(qe[:, c, of_image(i)], bank_c.t[:, of_image(i)], ACT.Exp,
                                             bias=bq_less[:, c, i:i + 1], accum_out=sq[:, c, i:i + 1]
                                             ).then_inc(bank_c.emptied.sem, 1)
                    for i in range(2):
                        p = pair_of(t, u, L1_CTX[i])
                        if p is not None:
                            act.wait_ge(bank_c.filled.sem, bank_c.full(p, f"ctx{i}"))
                            act.wait_ge(q_rsum.sem, q_rsum.at(p, KC))
                            for c in range(KC):
                                s.activation(cx[:, i, c], bank_c.t[:, c * CH:(c + 1) * CH], ACT.Copy,
                                             scale=rq[:, c, i:i + 1]).then_inc(bank_c.emptied.sem, 1)
                    for c in range(KC):
                        p = pair_of(t, u, L2_QK[c][0])
                        if p is not None:
                            act.wait_ge(bank_d.filled.sem, bank_d.full(p, f"q{c}"))
                            s.activation(q2[:, c], bank_d.t[:, 0:N2], ACT.Identity, bias=qb2s[:, c:c + 1], scale=SCALE2
                                         ).then_inc(bank_d.emptied.sem, 1)
                        p = pair_of(t, u, L2_QK[c][1])
                        if p is not None:
                            act.wait_ge(bank_d.filled.sem, bank_d.full(p, f"k{c}"))
                            s.activation(k2[:, c], bank_d.t[:, 0:N2], ACT.Identity, bias=w["kb2"][:, c:c + 1]
                                         ).then_inc(bank_d.emptied.sem, 1)
                    for i in range(2):
                        p = pair_of(t, u, L2_V[i])
                        if p is not None:
                            act.wait_ge(bank_d.filled.sem, bank_d.full(p, f"v{i}"))
                            s.copy(v2[:, i].rearrange("p c n -> p (c n)"), bank_d.t[0:HALF, :]).then_inc(bank_d.emptied.sem, 1)
                    for j in range(4):
                        p = pair_of(t, u, L3_V[j])
                        if p is not None:
                            act.wait_ge(bank_e.filled.sem, bank_e.full(p, f"v{j}"))
                            s.copy(v3t[:, j], bank_e.t[0:HALF, 0:CH + 1]).then_inc(bank_e.emptied.sem, 1)
                    for c in range(KC):
                        p = pair_of(t, u, L3_Q[c])
                        if p is not None:
                            act.wait_ge(bank_e.filled.sem, bank_e.full(p, f"q{c}"))
                            s.activation(qt3[:, c], bank_e.t[:, 0:N2], ACT.Identity, bias=qu3[:, c:c + 1]
                                         ).then_inc(bank_e.emptied.sem, 1)
                    for i in range(2):
                        p = pair_of(t, u, L3_S[i])
                        if p is not None:
                            act.wait_ge(l3_less_steps.sem, l3_less_steps.at(p, 5 * (i + 1)))
                            act.wait_ge(p3_done.sem, p3_done.at(p, 0))
                            for tc in range(2):
                                j = 2 * i + tc
                                s.activation(e3[:, j], bank_e.t[0:HALF, of_image(tc)], ACT.Exp, scale=SCALE3,
                                             bias=nm3[:, j:j + 1], accum_out=s3[:, j:j + 1]
                                             ).then_inc(bank_e.emptied.sem, 1)
                        p = pair_of(t, u, L3_T[i])
                        if p is not None:
                            act.wait_ge(bank_e.filled.sem, bank_e.full(p, f"t{i}"))
                            s.copy(pt3[:, i].rearrange("p c n -> p (c n)"), bank_e.t[0:HALF, 0:N2]
                                   ).then_inc(bank_e.emptied.sem, 1)
            run(act, step)

        @block.vector
        def _(dve):
            v = nc.vector

            def rsqrt(link, x, half, y, tmp):
                link(v.tensor_scalar(half, x, -0.5, None, ALU.mult))
                link(v.tensor_scalar(y.bitcast(I32), x.bitcast(I32), -0.5, MAGIC, ALU.mult, ALU.add))
                for _ in range(NEWTON):
                    link(v.tensor_tensor(tmp, y, y, ALU.mult))
                    link(v.tensor_tensor(tmp, tmp, half, ALU.mult))
                    link(v.scalar_tensor_tensor(out=y, in0=tmp, scalar=1.5, in1=y, op0=ALU.add, op1=ALU.mult))

            dve.wait_ge(weights_in, WEIGHTS)
            bn_done = [0]

            def bn_link(ins):
                bn_done[0] += 1
                ins.then_inc(bn_steps, 1)
                dve.wait_ge(bn_steps, bn_done[0])
            bn_link(v.tensor_scalar(bn_v[:], w["bn_v"][:], EPS, None, ALU.add))
            rsqrt(bn_link, bn_v[:], bn_half[:], bn_y[:], bn_t[:])
            bn_link(v.tensor_tensor(bn_scale[:], bn_y[:], w["bn_g"][:], ALU.mult))
            bn_link(v.tensor_tensor(bn_t[:], bn_scale[:], w["bn_m"][:], ALU.mult))
            bn_link(v.tensor_tensor(bn_shift[:], w["bn_b"][:], bn_t[:], ALU.subtract))
            bn_link(v.tensor_scalar(qb2s[:], w["qb2"][:], SCALE2, None, ALU.mult))
            assert bn_done[0] == BN_STEPS
            dve.wait_ge(fold_filled, FOLDS)
            folded = [
                v.tensor_copy(kv1[:, 0, CH:2 * CH], bank_a.t[:, 0:CH]),
                v.tensor_copy(kv1[:, 1, CH:2 * CH], bank_a.t[:, CH:2 * CH]),
                v.tensor_copy(kvb1[:, CH:2 * CH], ps_b[0:HALF, 0:CH]),
                v.tensor_copy(q3[:, 0], bank_c.t[:, 0:CH]),
                v.tensor_copy(q3[:, 1], bank_c.t[:, CH:2 * CH]),
                v.tensor_copy(v3[:, 0], bank_d.t[:, 0:CH + 1]),
                v.tensor_copy(v3[:, 1], bank_e.t[:, 0:CH + 1]),
                v.tensor_tensor(pb2[:], bank_s.t[:, 0:KC], w["pb2"][:], ALU.add),
                v.tensor_copy(qu3[:], bank_s.t[:, 2:2 + KC]),
                v.tensor_tensor(ob3[:], bank_s.t[:, 4:4 + KC], w["ob3"][:], ALU.add),
                v.tensor_copy(bqk3[:], bank_s.t[0:HALF, 6:7]),
            ]
            for ins in folded:
                ins.then_inc(fold_emptied, 1)
            dve.wait_ge(fold_emptied, FOLD_COPIES)

            def group_stats(p, n, src, bank):
                t = gn[n]
                link = linker(dve, t.stat_steps, p, 8)
                dve.wait_ge(bank.filled.sem, bank.filled.at(p, 0))
                for j in range(4):
                    v.bn_stats(t.stats[:, j], src[:, j // 2, of_image(j % 2)]).then_inc(t.stat_steps.sem, 1)
                for j in range(4):
                    dve.wait_ge(t.stat_steps.sem, t.stat_steps.at(p, j + 1))
                    dve.sem_inc(dve_held, 1)
                    v.bn_aggr(t.mine[:, :, j], t.stats[:, j]).then_inc(t.stat_steps.sem, 1)
                dve.wait_ge(t.stat_steps.sem, t.stat_steps.at(p, 8))
                link(v.tensor_tensor(t.sq[:], t.mine[:, 0], t.mine[:, 0], ALU.mult))
                v.tensor_tensor(t.mine[:, 1], t.mine[:, 1], t.sq[:], ALU.add).then_inc(t.stats_ready.sem, 1)

            def group_means(p, n, bank):
                t = gn[n]
                dve.wait_ge(bank.filled.sem, bank.full(p, "gn"))
                dve.wait_ge(t.steps.sem, t.steps.at(p, 0))
                v.tensor_copy(t.group[:], bank.t[:, 0:8].rearrange("p (a b) -> p a b", a=2)).then_inc(bank.emptied.sem, 1)

            def step(t):
                for u in range(SLOTS):
                    for n in range(UNITS):
                        p = pair_of(t, u, ATT + n)
                        if p is not None:
                            dve.wait_ge(bank_s.filled.sem, bank_s.full(p, n))
                            v.tensor_reduce(out=nm2[:, n % 2], in_=bank_s.t[0:HALF, 0:N2].rearrange("p (c n) -> p c n", c=2),
                                            axis=AX.X, op=ALU.max, negate=True).then_inc(max2_done.sem, 1)
                    for n in range(0, UNITS, 2):
                        p = pair_of(t, u, ATT + n + 1)
                        if p is not None:
                            dve.wait_ge(bank_t.filled.sem, bank_t.full(p, n))
                            dve.wait_ge(bank_o.filled.sem, bank_o.filled.at(p, max(n - 1, 0)))
                            v.tensor_copy(turned(n), bank_t.t[0:HALF, 0:N2]).then_inc(bank_t.emptied.sem, 1)
                    for i in range(2):
                        p = pair_of(t, u, L0_S[i])
                        if p is not None:
                            dve.wait_ge(bank_a.filled.sem, bank_a.full(p, f"s{i}"))
                            v.tensor_tensor(s0[:, i].rearrange("p (i j) n -> p i j n", i=2),
                                            bank_a.t[0:HALF, 0:8 * T7].rearrange("p (i j n) -> p i j n", i=2, j=4),
                                            w["bias0"][:, i].unsqueeze(1).broadcast_to([HALF, 2, 4, T7]),
                                            ALU.add).then_inc(bank_a.emptied.sem, 1)
                            dve.wait_ge(bank_a.emptied.sem, bank_a.read(p, f"s{i}"))
                            link = linker(dve, l0_soft_steps, p, 4 * i)
                            link(v.tensor_reduce(out=m0[:, i], in_=s0[:, i], axis=AX.X, op=ALU.max, negate=True))
                            v.tensor_tensor(s0[:, i], s0[:, i], m0[:, i].unsqueeze(2).broadcast_to([HALF, 8, T7]),
                                            ALU.add).then_inc(l0_soft_steps.sem, 1)
                        p = pair_of(t, u, L0_SUM[i])
                        if p is not None:
                            dve.wait_ge(l0_exp_done.sem, l0_exp_done.at(p, i + 1))
                            dve.wait_ge(l0_probs.sem, l0_probs.at(p, i))
                            link = linker(dve, l0_soft_steps, p, 4 * i + 2)
                            link(v.tensor_reduce(out=d0[:, i], in_=e0[:, i], axis=AX.X, op=ALU.add))
                            v.reciprocal(r0[:, i], d0[:, i]).then_inc(l0_soft_steps.sem, 1)
                    for k in range(9):
                        p = pair_of(t, u, CONV1[k])
                        if p is not None:
                            for c in range(KC):
                                dst, tap = y1[:, c, 0:CR], w["dw1"][:, c, k:k + 1]
                                if k == 0:
                                    dve.wait_ge(bn1_done.sem, bn1_done.at(p, c + 1))
                                    if has_before(p):
                                        dve.wait_ge(bank_a.emptied.sem, bank_a.read(p - 1, "q1"))
                                        dve.wait_ge(resize_steps.sem, resize_steps.at(p, 0))
                                    v.tensor_scalar(dst, window(xpad, c, k), tap, None, ALU.mult).then_inc(conv1_steps.sem, 1)
                                else:
                                    dve.wait_ge(conv1_steps.sem, conv1_steps.at(p, KC * (k - 1) + c + 1))
                                    v.scalar_tensor_tensor(out=dst, in0=window(xpad, c, k), scalar=tap, in1=dst,
                                                           op0=ALU.mult, op1=ALU.add).then_inc(conv1_steps.sem, 1)
                    for k in range(9):
                        p = pair_of(t, u, CONV2[k])
                        if p is not None:
                            for c in range(KC):
                                dst, tap = y2[:, c, 0:CR], w["dw2"][:, c, k:k + 1]
                                if k == 0:
                                    dve.wait_ge(bank_a.emptied.sem, bank_a.read(p, "o1"))
                                    dve.wait_ge(bank_b.emptied.sem, bank_b.free(p, "pw0"))
                                    v.tensor_scalar(dst, window(opad, c, k), tap, None, ALU.mult).then_inc(conv2_steps.sem, 1)
                                else:
                                    dve.wait_ge(conv2_steps.sem, conv2_steps.at(p, KC * (k - 1) + c + 1))
                                    v.scalar_tensor_tensor(out=dst, in0=window(opad, c, k), scalar=tap, in1=dst,
                                                           op0=ALU.mult, op1=ALU.add).then_inc(conv2_steps.sem, 1)
                    for c in range(KC):
                        p = pair_of(t, u, L0_PW[c])
                        if p is not None:
                            dve.wait_ge(bank_b.filled.sem, bank_b.full(p, f"pw{c}"))
                            dve.wait_ge(res_loaded.sem, res_loaded.at(p, 16))
                            dve.wait_ge(act0_done.sem, act0_done.at(p, 0))
                            v.tensor_tensor(res0[:, c], bank_b.t[:, 0:N2], x_res[:, c], ALU.add
                                            ).then_inc(bank_b.emptied.sem, 1)
                        p = pair_of(t, u, L0_MLP[c])
                        if p is not None:
                            dve.wait_ge(bank_b.filled.sem, bank_b.full(p, f"mlp{c}"))
                            dve.wait_ge(gn[1].done.sem, gn[1].done.at(p, 0))
                            v.tensor_tensor(x1[:, c], bank_b.t[:, 0:N2], res0[:, c], ALU.add
                                            ).then_inc(bank_b.emptied.sem, 1)
                    p = pair_of(t, u, GN1[0])
                    if p is not None:
                        dve.wait_ge(bank_b.emptied.sem, bank_b.read(p, "mlp1"))
                        group_stats(p, 1, x1, bank_b)
                    p = pair_of(t, u, GN1[1])
                    if p is not None:
                        group_means(p, 1, bank_b)
                    for j in range(4):
                        p = pair_of(t, u, L1_KV[j])
                        if p is not None:
                            dve.wait_ge(bank_c.filled.sem, bank_c.full(p, f"kv{j}"))
                            v.tensor_tensor(kv[:, j], bank_c.t[0:HALF, :], kvb1[:], ALU.add).then_inc(bank_c.emptied.sem, 1)
                            dve.wait_ge(bank_c.emptied.sem, bank_c.read(p, f"kv{j}"))
                            v.tensor_reduce(out=nmk[:, j:j + 1], in_=kv[:, j, 0:CH], axis=AX.X, op=ALU.max, negate=True
                                            ).then_inc(k_less.sem, 1)
                        p = pair_of(t, u, L1_KV[j] + 1)
                        if p is not None:
                            dve.wait_ge(k_exp_done.sem, k_exp_done.at(p, j + 1))
                            dve.wait_ge(k_scaled.sem, k_scaled.at(p, 0))
                            v.reciprocal(rk[:, j:j + 1], sk[:, j:j + 1]).then_inc(k_rsum.sem, 1)
                    for c in range(KC):
                        p = pair_of(t, u, L1_Q[c])
                        if p is not None:
                            dve.wait_ge(bank_c.filled.sem, bank_c.full(p, f"q{c}"))
                            link = linker(dve, q_less_steps, p, 3 * c)
                            link(v.tensor_reduce(out=mq[:, c], in_=bank_c.t[:, 0:N2].rearrange("p (i n) -> p i n", i=2),
                                                 axis=AX.X, op=ALU.max))
                            link(v.tensor_scalar(mqb[:, c], mq[:, c], w["qb1"][:, c:c + 1], -1.0, ALU.add, ALU.mult))
                            v.tensor_scalar(bq_less[:, c], mqb[:, c], w["qb1"][:, c:c + 1], None, ALU.add
                                            ).then_inc(q_less_steps.sem, 1)
                        p = pair_of(t, u, L1_Q[c] + 1)
                        if p is not None:
                            dve.wait_ge(bank_c.emptied.sem, bank_c.read(p, f"q{c}"))
                            v.reciprocal(rq[:, c], sq[:, c]).then_inc(q_rsum.sem, 1)
                    for c in range(KC):
                        p = pair_of(t, u, L1_OUT[c])
                        if p is not None:
                            dve.wait_ge(bank_c.filled.sem, bank_c.full(p, f"out{c}"))
                            dve.wait_ge(gn[2].done.sem, gn[2].done.at(p, 0))
                            dve.wait_ge(hop_a_done.sem, hop_a_done.at(p, 0))
                            v.scalar_tensor_tensor(out=x2[:, c], in0=bank_c.t[:, 0:N2], scalar=w["pb1"][:, c:c + 1],
                                                   in1=xn1[:, c], op0=ALU.add, op1=ALU.add
                                                   ).then_inc(bank_c.emptied.sem, 1)
                    p = pair_of(t, u, L2_RDEN)
                    if p is not None:
                        dve.wait_ge(bank_s.emptied.sem, bank_s.read(p, UNITS - 1))
                        dve.wait_ge(bank_n.filled.sem, bank_n.filled.at(p, 0))
                        v.reciprocal(rden2[:], den2[:]).then_inc(rden_done.sem, 1)
                    p = pair_of(t, u, L2_RT)
                    if p is not None:
                        dve.wait_ge(bank_n.filled.sem, bank_n.full(p, "rt"))
                        v.tensor_copy(rt2[:], bank_n.t[0:H2, 0:N2]).then_inc(bank_n.emptied.sem, 1)
                    for i in range(2):
                        p = pair_of(t, u, L2_REP[i])
                        if p is not None:
                            dve.wait_ge(bank_n.filled.sem, bank_n.full(p, f"rep{i}"))
                            dve.wait_ge(bank_o.emptied.sem, bank_o.emptied.at(p, i + 1))
                            v.tensor_tensor(a2[:, i].rearrange("p c n -> p (c n)"), bank_n.t[:, 0:N2],
                                            araw[:, i].rearrange("p c n -> p (c n)"), ALU.mult
                                            ).then_inc(bank_n.emptied.sem, 1)
                    for c in range(KC):
                        p = pair_of(t, u, L2_PROJ[c])
                        if p is not None:
                            dve.wait_ge(bank_n.filled.sem, bank_n.full(p, f"proj{c}"))
                            dve.wait_ge(hop_b_done.sem, hop_b_done.at(p, 16))
                            dve.wait_ge(gn[3].done.sem, gn[3].done.at(p, 0))
                            dve.wait_ge(bank_e.emptied.sem, bank_e.free(p, "v0"))
                            v.scalar_tensor_tensor(out=x3[:, c], in0=bank_n.t[:, 0:N2], scalar=pb2[:, c:c + 1],
                                                   in1=x2b[:, c], op0=ALU.add, op1=ALU.add
                                                   ).then_inc(bank_n.emptied.sem, 1)
                    p = pair_of(t, u, GN2[0])
                    if p is not None:
                        dve.wait_ge(bank_c.emptied.sem, bank_c.read(p, "out1"))
                        group_stats(p, 2, x2, bank_d)
                    p = pair_of(t, u, GN2[1])
                    if p is not None:
                        group_means(p, 2, bank_d)
                    p = pair_of(t, u, GN3[0])
                    if p is not None:
                        dve.wait_ge(bank_n.emptied.sem, bank_n.read(p, "proj1"))
                        group_stats(p, 3, x3, bank_n)
                    p = pair_of(t, u, GN3[1])
                    if p is not None:
                        group_means(p, 3, bank_n)
                    for i in range(2):
                        p = pair_of(t, u, L3_S[i])
                        if p is not None:
                            both = slice(2 * i, 2 * i + 2)
                            dve.wait_ge(bank_e.filled.sem, bank_e.full(p, f"s{i}"))
                            link = linker(dve, l3_less_steps, p, 5 * i)
                            link(v.tensor_scalar(rb3[:, both], v3t[:, both, CH], bqk3[:, 0:1], None, ALU.add))
                            link(v.tensor_reduce(out=m3[:, both], in_=bank_e.t[0:HALF, 0:N2].rearrange("p (c n) -> p c n", c=2),
                                                 axis=AX.X, op=ALU.max))
                            link(v.tensor_tensor(t3[:, both], m3[:, both], rb3[:, both], ALU.add))
                            link(v.tensor_tensor(u3[:, both], rb3[:, both], t3[:, both], ALU.subtract))
                            v.tensor_scalar(nm3[:, both], u3[:, both], SCALE3, None, ALU.mult).then_inc(l3_less_steps.sem, 1)
                        p = pair_of(t, u, L3_S[i] + 1)
                        if p is not None:
                            dve.wait_ge(bank_e.emptied.sem, bank_e.read(p, f"s{i}"))
                            dve.wait_ge(p3_done.sem, p3_done.at(p, 0))
                            v.reciprocal(r3[:, 2 * i:2 * i + 2], s3[:, 2 * i:2 * i + 2]).then_inc(l3_rsum.sem, 1)
                    for i in range(2):
                        p = pair_of(t, u, L3_O[i])
                        if p is not None:
                            dve.wait_ge(bank_e.filled.sem, bank_e.full(p, f"o{i}"))
                            dve.wait_ge(stored.sem, stored.at(p, 0))
                            for m in range(KC):
                                v.scalar_tensor_tensor(out=out[:, m, of_image(i)], in0=bank_e.t[:, of_image(m)],
                                                       scalar=ob3[:, m:m + 1], in1=x3[:, m, of_image(i)],
                                                       op0=ALU.add, op1=ALU.add).then_inc(bank_e.emptied.sem, 1)
            run(dve, step)

        @block.tensor
        def _(pe):
            def mm(dst, lhsT, rhs, start, stop):
                return nc.tensor.matmul(dst, lhsT, rhs, start=start, stop=stop)

            def product(dst, lhsT, rhs, ks=KC):
                for k in range(ks):
                    ins = mm(dst, lhsT(k), rhs(k), k == 0, k == ks - 1)
                return ins

            eye = w["eye"]
            pe.wait_ge(weights_in, WEIGHTS)
            for m in range(KC):
                last = product(bank_a.t[:, m * CH:(m + 1) * CH], lambda k: w["v1"][:, k, of_chunk(m)], lambda k: w["p1"][:, k])
            last.then_inc(fold_filled, 1)
            product(ps_b[0:HALF, 0:CH], lambda k: w["vb1_rep"][:, k], lambda k: w["p1"][:, k]).then_inc(fold_filled, 1)
            for m in range(KC):
                last = product(bank_c.t[:, m * CH:(m + 1) * CH], lambda k: w["q3"][:, k, of_chunk(m)], lambda k: w["k3"][:, k])
            last.then_inc(fold_filled, 1)
            for m, t in enumerate((bank_d.t, bank_e.t)):
                product(t[:, 0:CH], lambda k: w["v3"][:, k, of_chunk(m)], lambda k: w["o3"][:, k])
                product(t[:, CH:CH + 1], lambda k: w["q3"][:, k, of_chunk(m)], lambda k: w["kb3"][:, k:k + 1]
                        ).then_inc(fold_filled, 1)
            for m in range(KC):
                product(bank_s.t[:, m:m + 1], lambda k: w["p2"][:, k, of_chunk(m)], lambda k: w["vb2"][:, k:k + 1])
                product(bank_s.t[:, 2 + m:3 + m], lambda k: w["k3"][:, k, of_chunk(m)], lambda k: w["qb3"][:, k:k + 1])
                product(bank_s.t[:, 4 + m:5 + m], lambda k: w["o3"][:, k, of_chunk(m)], lambda k: w["vb3"][:, k:k + 1])
            product(bank_s.t[0:HALF, 6:7], lambda k: w["qb3_rep"][:, k], lambda k: w["kb3"][:, k:k + 1]).then_inc(fold_filled, 1)
            pe.wait_ge(fold_emptied, FOLD_COPIES)
            pe.wait_ge(consts_set, CONSTS)

            def scores2(p, n):
                i, c, r = n // H2, (n % H2) // 4, 32 * (n % 4)
                pe.wait_ge(bank_s.emptied.sem, bank_s.free(p, n))
                if n == 0:
                    pe.wait_ge(bank_d.emptied.sem, bank_d.read(p, "k0"))
                if n == 4:
                    pe.wait_ge(bank_d.emptied.sem, bank_d.read(p, "k1"))
                for tc in range(2):
                    last = mm(bank_s.t[0:HALF, of_image(tc)], q2[r:r + 32, c, of_tile(i, tc)],
                              k2[r:r + 32, c, of_image(i)], True, True)
                last.then_inc(bank_s.filled.sem, 1)

            def turn2(p, n):
                pe.wait_ge(bank_t.emptied.sem, bank_t.free(p, n))
                pe.wait_ge(bank_s.emptied.sem, bank_s.read(p, n))
                for tc in range(2):
                    for sc in range(2):
                        last = nc.tensor.transpose(bank_t.t[0:HALF, of_tile(sc, tc)],
                                                   e2[:, n % 2, tc, sc * HALF:(sc + 1) * HALF], eye[0:HALF, 0:HALF])
                last.then_inc(bank_t.filled.sem, 1)

            def values2(p, n):
                i, h = n // H2, n % H2
                c, r = h // 4, 32 * (h % 4)
                if h == 0:
                    pe.wait_ge(bank_o.emptied.sem, bank_o.free(p, i))
                    pe.wait_ge(bank_d.emptied.sem, bank_d.read(p, f"v{i}"))
                pe.wait_ge(bank_t.emptied.sem, bank_t.read(p, n))
                product(bank_o.t[r:r + 32, of_image(c)], lambda sc: v2[:, i, sc, 32 * h:32 * h + 32],
                        lambda sc: pt2[:, n % 2, sc]).then_inc(bank_o.filled.sem, 1)

            def step(t):
                for u in range(SLOTS):
                    for n in range(UNITS):
                        p = pair_of(t, u, ATT + n + 1)
                        if p is not None:
                            turn2(p, n)
                    for n in range(UNITS):
                        p = pair_of(t, u, ATT + n)
                        if p is not None:
                            scores2(p, n)
                    for c in range(KC):
                        p = pair_of(t, u, L0_Q[c])
                        if p is not None:
                            pe.wait_ge(bank_a.emptied.sem, bank_a.free(p, f"q{c}"))
                            pe.wait_ge(conv1_steps.sem, conv1_steps.at(p, KC * 9))
                            product(bank_a.t[:, 0:N2], lambda k: w["q0"][:, k, of_chunk(c)],
                                    lambda k: y1[:, k].rearrange("p (i r) n -> p i (r n)", i=2)[:, :, 0:TOK]
                                    ).then_inc(bank_a.filled.sem, 1)
                    p = pair_of(t, u, L0_K)
                    if p is not None:
                        pe.wait_ge(bank_a.emptied.sem, bank_a.free(p, "k"))
                        pe.wait_ge(resize_steps.sem, resize_steps.at(p, 9 * KC))
                        for m in range(2):
                            last = product(bank_a.t[:, 2 * T7 * m:2 * T7 * (m + 1)], lambda k: w["k0"][:, k, of_chunk(m)],
                                           lambda k: yr[:, k, :, 0, 0:T7])
                        last.then_inc(bank_a.filled.sem, 1)
                    p = pair_of(t, u, L0_V)
                    if p is not None:
                        pe.wait_ge(bank_a.emptied.sem, bank_a.free(p, "v"))
                        for i in range(2):
                            last = product(bank_a.t[:, i * CH:(i + 1) * CH],
                                           lambda k: yr[:, k, i].rearrange("p a n -> p (a n)"), lambda k: w["v0"][:, k])
                        last.then_inc(bank_a.filled.sem, 1)
                    for i in range(2):
                        p = pair_of(t, u, L0_S[i])
                        if p is not None:
                            pe.wait_ge(bank_a.emptied.sem, bank_a.free(p, f"s{i}"))
                            r = 64 * i
                            for j in range(8):
                                image, tc, m = j // 4, j // 2 % 2, j % 2
                                last = mm(bank_a.t[0:HALF, j * T7:(j + 1) * T7], q0[r:r + 64, m, of_tile(image, tc)],
                                          k0[r:r + 64, m, image], True, True)
                            last.then_inc(bank_a.filled.sem, 1)
                        p = pair_of(t, u, L0_T[i])
                        if p is not None:
                            pe.wait_ge(bank_a.emptied.sem, bank_a.free(p, f"t{i}"))
                            pe.wait_ge(l0_probs.sem, l0_probs.at(p, 2))
                            for tc in range(2):
                                for m in range(2):
                                    last = nc.tensor.transpose(bank_a.t[:, of_tile(m, tc)],
                                                               p0[:, 4 * i + 2 * tc + m].rearrange("p h n -> p (h n)"),
                                                               eye[0:HALF, 0:HALF])
                            last.then_inc(bank_a.filled.sem, 1)
                        p = pair_of(t, u, L0_O[i])
                        if p is not None:
                            pe.wait_ge(bank_a.emptied.sem, bank_a.free(p, f"o{i}"))
                            for m in range(2):
                                last = mm(bank_a.t[:, of_image(m)], v0[:, i, m], pt0[:, i, m], True, True)
                            last.then_inc(bank_a.filled.sem, 1)
                    for c in range(KC):
                        p = pair_of(t, u, L0_PW[c])
                        if p is not None:
                            if c == 0 and not (isinstance(p, int) and p < 3):
                                pe.wait_ge(bank_n.emptied.sem, bank_n.free(p - 2, "rt"))
                            pe.wait_ge(bank_b.emptied.sem, bank_b.free(p, f"pw{c}"))
                            pe.wait_ge(conv2_steps.sem, conv2_steps.at(p, KC * 9))
                            product(bank_b.t[:, 0:N2], lambda k: w["o0"][:, k, of_chunk(c)],
                                    lambda k: y2[:, k].rearrange("p (i r) n -> p i (r n)", i=2)[:, :, 0:TOK]
                                    ).then_inc(bank_b.filled.sem, 1)
                        p = pair_of(t, u, L0_MLP[c])
                        if p is not None:
                            pe.wait_ge(bank_b.emptied.sem, bank_b.free(p, f"mlp{c}"))
                            pe.wait_ge(act0_done.sem, act0_done.at(p, KC))
                            product(bank_b.t[:, 0:N2], lambda k: w["mlp0"][:, k, of_chunk(c)],
                                    lambda k: act0[:, k]).then_inc(bank_b.filled.sem, 1)
                    for n, stage, bank, group in ((1, GN1, bank_b, "group32"), (2, GN2, bank_d, "group8"),
                                                  (3, GN3, bank_n, "group8")):
                        p = pair_of(t, u, stage[1])
                        if p is not None:
                            pe.wait_ge(bank.emptied.sem, bank.free(p, "gn"))
                            pe.wait_ge(gn[n].stats_ready.sem, gn[n].stats_ready.at(p, 1))
                            mm(bank.t[:, 0:8], w[group][:], gn[n].mine[:].rearrange("p a b -> p (a b)"), True, True
                               ).then_inc(bank.filled.sem, 1)
                    for j in range(4):
                        p = pair_of(t, u, L1_KV[j])
                        if p is not None:
                            pe.wait_ge(bank_c.emptied.sem, bank_c.free(p, f"kv{j}"))
                            pe.wait_ge(gn[1].done.sem, gn[1].done.at(p, 4))
                            product(bank_c.t[0:HALF, :], lambda k: xn1[:, k, of_tile(j // 2, j % 2)],
                                    lambda k: kv1[:, k]).then_inc(bank_c.filled.sem, 1)
                    for c in range(KC):
                        p = pair_of(t, u, L1_Q[c])
                        if p is not None:
                            pe.wait_ge(bank_c.emptied.sem, bank_c.free(p, f"q{c}"))
                            product(bank_c.t[:, 0:N2], lambda k: w["q1"][:, k, of_chunk(c)], lambda k: xn1[:, k]
                                    ).then_inc(bank_c.filled.sem, 1)
                    for i in range(2):
                        p = pair_of(t, u, L1_CTX[i])
                        if p is not None:
                            pe.wait_ge(bank_c.emptied.sem, bank_c.free(p, f"ctx{i}"))
                            pe.wait_ge(k_scaled.sem, k_scaled.at(p, 2 * (i + 1)))
                            for c in range(KC):
                                last = product(bank_c.t[:, c * CH:(c + 1) * CH], lambda k: kn[:, 2 * i + k, of_chunk(c)],
                                               lambda k: kv[:, 2 * i + k, CH:2 * CH])
                            last.then_inc(bank_c.filled.sem, 1)
                    for c in range(KC):
                        p = pair_of(t, u, L1_OUT[c])
                        if p is not None:
                            pe.wait_ge(bank_c.emptied.sem, bank_c.free(p, f"out{c}"))
                            for i in range(2):
                                last = product(bank_c.t[:, of_image(i)], lambda k: cx[:, i, k, of_chunk(c)],
                                               lambda k: qe[:, k, of_image(i)])
                            last.then_inc(bank_c.filled.sem, 1)
                    for c in range(KC):
                        for name, start in zip(("q", "k"), L2_QK[c]):
                            p = pair_of(t, u, start)
                            if p is not None:
                                pe.wait_ge(bank_d.emptied.sem, bank_d.free(p, f"{name}{c}"))
                                pe.wait_ge(gn[2].done.sem, gn[2].done.at(p, 4))
                                product(bank_d.t[:, 0:N2], lambda k: w[f"{name}2"][:, k, of_chunk(c)],
                                        lambda k: xn2[:, k]).then_inc(bank_d.filled.sem, 1)
                    for i in range(2):
                        p = pair_of(t, u, L2_V[i])
                        if p is not None:
                            pe.wait_ge(bank_d.emptied.sem, bank_d.free(p, f"v{i}"))
                            for tc in range(2):
                                last = product(bank_d.t[0:HALF, tc * CH:(tc + 1) * CH], lambda k: xn2[:, k, of_tile(i, tc)],
                                               lambda k: w["v2"][:, k])
                            last.then_inc(bank_d.filled.sem, 1)
                    for n in range(UNITS):
                        p = pair_of(t, u, ATT + n + 2)
                        if p is not None:
                            values2(p, n)
                    p = pair_of(t, u, L2_RT)
                    if p is not None:
                        pe.wait_ge(bank_b.emptied.sem, bank_b.free(min(p + 3, PAIRS) if isinstance(p, int) else p + 3, "pw0"))
                        pe.wait_ge(bank_n.emptied.sem, bank_n.free(p, "rt"))
                        pe.wait_ge(rden_done.sem, rden_done.at(p, 1))
                        for j in range(4):
                            last = nc.tensor.transpose(bank_n.t[0:H2, j * HALF:(j + 1) * HALF], rden2[:, j],
                                                       eye[0:HALF, 0:HALF])
                        last.then_inc(bank_n.filled.sem, 1)
                    for i in range(2):
                        p = pair_of(t, u, L2_REP[i])
                        if p is not None:
                            pe.wait_ge(bank_n.emptied.sem, bank_n.free(p, f"rep{i}"))
                            for c in range(KC):
                                last = mm(bank_n.t[:, of_image(c)], w["heads"][:, c], rt2[:, of_image(i)], True, True)
                            last.then_inc(bank_n.filled.sem, 1)
                    for c in range(KC):
                        p = pair_of(t, u, L2_PROJ[c])
                        if p is not None:
                            pe.wait_ge(bank_n.emptied.sem, bank_n.free(p, f"proj{c}"))
                            product(bank_n.t[:, 0:N2], lambda k: w["p2"][:, k, of_chunk(c)], lambda k: a2[:, :, k]
                                    ).then_inc(bank_n.filled.sem, 1)
                    for j in range(4):
                        p = pair_of(t, u, L3_V[j])
                        if p is not None:
                            pe.wait_ge(bank_e.emptied.sem, bank_e.free(p, f"v{j}"))
                            pe.wait_ge(gn[3].done.sem, gn[3].done.at(p, 4))
                            product(bank_e.t[0:HALF, 0:CH + 1], lambda k: xn3[:, k, of_tile(j // 2, j % 2)],
                                    lambda k: v3[:, k]).then_inc(bank_e.filled.sem, 1)
                    for c in range(KC):
                        p = pair_of(t, u, L3_Q[c])
                        if p is not None:
                            pe.wait_ge(bank_e.emptied.sem, bank_e.free(p, f"q{c}"))
                            product(bank_e.t[:, 0:N2], lambda k: q3[:, k, of_chunk(c)], lambda k: xn3[:, k]
                                    ).then_inc(bank_e.filled.sem, 1)
                    for i in range(2):
                        p = pair_of(t, u, L3_S[i])
                        if p is not None:
                            pe.wait_ge(bank_e.emptied.sem, bank_e.free(p, f"s{i}"))
                            for tc in range(2):
                                last = product(bank_e.t[0:HALF, of_image(tc)], lambda k: qt3[:, k, of_tile(i, tc)],
                                               lambda k: xn3[:, k, of_image(i)])
                            last.then_inc(bank_e.filled.sem, 1)
                        p = pair_of(t, u, L3_T[i])
                        if p is not None:
                            pe.wait_ge(bank_e.emptied.sem, bank_e.free(p, f"t{i}"))
                            pe.wait_ge(p3_done.sem, p3_done.at(p, 2 * (i + 1)))
                            for tc in range(2):
                                for sc in range(2):
                                    last = nc.tensor.transpose(bank_e.t[0:HALF, of_tile(sc, tc)],
                                                               p3[:, 2 * i + tc, sc * HALF:(sc + 1) * HALF],
                                                               eye[0:HALF, 0:HALF])
                            last.then_inc(bank_e.filled.sem, 1)
                        p = pair_of(t, u, L3_O[i])
                        if p is not None:
                            pe.wait_ge(bank_e.emptied.sem, bank_e.free(p, f"o{i}"))
                            for m in range(KC):
                                last = product(bank_e.t[:, of_image(m)], lambda k: v3t[:, 2 * i + k, of_chunk(m)],
                                               lambda k: pt3[:, i, k])
                            last.then_inc(bank_e.filled.sem, 1)
            run(pe, step)


def rows(x):
    return np.ascontiguousarray(np.moveaxis(x.reshape(KC, 128, *x.shape[1:]), 0, 1))


def laid_out(v):
    z = {}
    both = lambda a, b: np.concatenate([rows(a), rows(b)], axis=1)
    twice = lambda a: np.repeat(rows(a), 2, axis=1)
    z["x"] = np.ascontiguousarray(
        v["x"].reshape(PAIRS, 2, KC, 128, TOK).transpose(0, 3, 2, 1, 4).reshape(PAIRS, 128, KC * N2))
    for q in "gbmv":
        z["bn_" + q] = both(v["L0_conv_bn1_" + q], v["L0_conv_bn2_" + q])
    z["dw1"] = rows(v["L0_conv_w_qkv_dw"].reshape(CH, 9))
    at = np.linspace(0.0, SIDE - 1, R7, dtype=np.float32)[:6]
    z["frac"] = np.broadcast_to((at - np.floor(at)).astype(np.float32), (128, 6)).copy()
    by_head = (np.arange(D0)[None, :] * H0 + np.arange(H0)[:, None]).reshape(-1)
    q, k, u = np.split(v["L0_conv_w_qkv_pw"], 3)
    z["q0"], z["k0"], z["v0"] = (rows(m[by_head].T) for m in (q, k, u))
    z["dw2"] = rows(v["L0_conv_w_out_dw"].reshape(CH, 9)[by_head])
    z["o0"] = rows(v["L0_conv_w_out_pw"].T[by_head])
    z["mlp0"] = rows(v["L0_conv_w_mlp"].T)
    table = v["L0_conv_rel_table"]
    side = 2 * R7 - 1
    r, c = np.arange(TOK) // SIDE // 2, np.arange(TOK) % SIDE // 2
    kr, kc = np.arange(T7) // R7, np.arange(T7) % R7
    at = (r[:, None] - kr[None] + R7 - 1) * side + (c[:, None] - kc[None] + R7 - 1)
    z["bias0"] = table[at].reshape(2, HALF, T7, 2, 2).transpose(1, 4, 0, 3, 2).reshape(HALF, 2, 4, T7)
    for n, size in ((32, 32), (8, 8)):
        z[f"group{n}"] = np.kron(np.eye(128 // size), np.full((size, size), 1.0 / size)).astype(np.float32)
    z["gn1_w"], z["gn1_b"] = twice(v["L1_conv_gn_w"]), twice(v["L1_conv_gn_b"])
    q, k, u = np.split(v["L1_conv_qkv_w"], 3)
    qb, kb, ub = np.split(v["L1_conv_qkv_b"], 3)
    z["q1"], z["qb1"], z["kv1"], z["v1"] = rows(q.T), rows(qb), rows(k.T), rows(u)
    z["kvb1"] = np.broadcast_to(kb, (HALF, CH))
    z["vb1_rep"] = np.broadcast_to(rows(ub)[:, :, None], (128, KC, HALF))
    z["p1"], z["pb1"] = rows(v["L1_conv_proj_w"].T), rows(v["L1_conv_proj_b"])
    z["gn2_w"], z["gn2_b"] = twice(v["L2_conv_norm_w"]), twice(v["L2_conv_norm_b"])
    q, k, u = v["L2_conv_qkv_w"].reshape(H2, 3, D2, CH).transpose(1, 0, 2, 3).reshape(3, CH, CH)
    qb, kb, ub = v["L2_conv_qkv_b"].reshape(H2, 3, D2).transpose(1, 0, 2).reshape(3, CH)
    z["q2"], z["k2"], z["v2"] = rows(q.T), rows(k.T), rows(u.T)
    z["qb2"], z["kb2"], z["vb2"] = rows(qb), rows(kb), rows(ub)
    z["p2"], z["pb2"] = rows(v["L2_conv_proj_w"].T), rows(v["L2_conv_proj_b"])
    z["heads"] = np.repeat(np.eye(H2), D2, axis=1).reshape(H2, KC, 128).astype(np.float32)
    z["eye"] = np.eye(128, dtype=np.float32)
    z["gn3_w"], z["gn3_b"] = twice(v["L3_conv_gamma"]), twice(v["L3_conv_beta"])
    z["q3"], z["k3"], z["v3"], z["o3"] = (rows(v["L3_conv_w" + m]) for m in "qkvo")
    z["o3"] = rows(v["L3_conv_wo"].T)
    z["qb3"], z["kb3"], z["vb3"], z["ob3"] = (rows(v["L3_conv_b" + m]) for m in "qkvo")
    z["qb3_rep"] = np.broadcast_to(rows(v["L3_conv_bq"])[:, :, None], (128, KC, HALF))
    return {name: np.ascontiguousarray(tile) for name, tile in z.items()}


def kernel(**inputs):
    import concourse.bacc as bacc
    from concourse.bass_utils import run_bass_kernel_spmd

    nc = bacc.Bacc("TRN2", target_bir_lowering=False, num_devices=1)
    arrays = {f"in_{k}": v for k, v in laid_out({k: np.asarray(v) for k, v in inputs.items()}).items()}
    a = {k[3:]: nc.dram_tensor(k, v.shape, mybir.dt.from_np(v.dtype), kind="ExternalInput").ap() for k, v in arrays.items()}
    a["out"] = nc.dram_tensor("out_pairs", (PAIRS, 128, KC * N2), F32, kind="ExternalOutput").ap()
    build(nc, a)
    r = run_bass_kernel_spmd(nc, [arrays], core_ids=[0])
    got = r.results[0]["out_pairs"].reshape(PAIRS, 128, KC, 2, TOK)
    return np.ascontiguousarray(got.transpose(0, 3, 2, 1, 4)).reshape(IMAGES, CH, SIDE, SIDE)
```

```python
import numpy as np
import concourse.bass as bass
from concourse import mybir
from contextlib import ExitStack

F32 = mybir.dt.float32
F32R = mybir.dt.float32r
I32 = mybir.dt.int32
ACT = mybir.ActivationFunctionType
ALU = mybir.AluOpType
AX = mybir.AxisListType

IMAGES, CH, SIDE = 64, 256, 14
TOK = SIDE * SIDE
HALF = TOK // 2
PAIRS = IMAGES // 2
KC = CH // 128
N2 = 2 * TOK
PAD = SIDE + 2
EPS = 1e-5
R7 = 7
T7 = R7 * R7
H0, D0 = 4, CH // 4
SCALE0 = D0 ** -0.5
H2, D2 = 8, CH // 8
SCALE2 = D2 ** -0.5
SCALE3 = CH ** -0.5
MAGIC = float(0x5F3759DF)
NEWTON = 3

SLOTS = 16
LOAD_X = -8
BN1 = (0, 1)
CONV1 = (1, 2, 4, 4, 5, 5, 6, 6, 6)
RESIZE = (7, 9)
L0_Q = (13, 14)
L0_K, L0_V = 15, 16
L0_S, L0_SUM = (17, 19), (18, 20)
L0_T, L0_O = (21, 22), (23, 24)
LOAD_RES = 23
CONV2 = (25, 26, 26, 27, 28, 29, 29, 30, 30)
L0_PW, L0_MLP = (31, 32), (34, 35)
GN1 = (35, 36, 36, 39)
L1_KV, L1_Q, L1_CTX, L1_OUT = (40, 41, 42, 43), (44, 45), (46, 47), (48, 49)
GN2 = (49, 50, 50, 52)
HOP = 62
L2_QK = ((53, 54), (57, 58))
L2_V = (55, 60)
ATT = 55
UNITS = 2 * H2
L2_RDEN, L2_RT, L2_REP, L2_PROJ = ATT + UNITS, 71, (72, 73), (73, 74)
GN3 = (76, 77, 77, 79)
HOP_OUT = 77
L3_V, L3_Q, L3_S, L3_T, L3_O = (81, 82, 83, 84), (85, 86), (87, 88), (89, 90), (91, 92)
STORE = 91
LAST_LAG = STORE // SLOTS


W_SHAPES = {
    "bn_g": (128, 4), "bn_b": (128, 4), "bn_m": (128, 4), "bn_v": (128, 4),
    "dw1": (128, KC, 9), "frac": (128, 6),
    "q0": (128, KC, CH), "k0": (128, KC, CH), "v0": (128, KC, CH), "bias0": (HALF, 2, 4, T7),
    "dw2": (128, KC, 9), "o0": (128, KC, CH), "mlp0": (128, KC, CH),
    "gn1_w": (128, 4), "gn1_b": (128, 4), "group32": (128, 128), "group8": (128, 128),
    "q1": (128, KC, CH), "qb1": (128, KC), "k1": (128, KC, CH), "kvb1": (HALF, 2 * CH),
    "v1": (128, KC, CH), "vb1_rep": (128, KC, HALF), "p1": (128, KC, CH), "pb1": (128, KC),
    "gn2_w": (128, 4), "gn2_b": (128, 4), "q2": (128, KC, CH), "k2": (128, KC, CH), "v2": (128, KC, CH),
    "qb2": (128, KC), "kb2": (128, KC), "vb2": (128, KC), "p2": (128, KC, CH), "pb2": (128, KC),
    "heads": (H2, KC, 128), "eye": (128, 128),
    "gn3_w": (128, 4), "gn3_b": (128, 4), "q3": (128, KC, CH), "k3": (128, KC, CH), "v3": (128, KC, CH),
    "o3": (128, KC, CH), "qb3": (128, KC), "kb3": (128, KC), "vb3": (128, KC), "ob3": (128, KC),
    "qb3_rep": (128, KC, HALF),
}
W_PARTS = {"kvb1": CH}
W_EARLY = ("k1", "q1", "v1", "vb1_rep", "p1", "q2", "k2", "v2", "vb2", "q3", "k3", "v3", "o3", "vb3", "qb3_rep")
SPLIT = {"kv1": 2 * CH, "q1": CH, "q2": CH, "k2": CH, "v2": CH, "v3": CH + 2, "q3": CH}


def build(nc, a):
    ctx = ExitStack()
    with ctx:
        def sb(name, shape, dt=F32):
            return ctx.enter_context(nc.sbuf_tensor(name, shape, dt))

        def sem(name):
            return ctx.enter_context(nc.semaphore(name))

        class Count:

            def __init__(self, name, per):
                self.sem, self.per = sem(name), per

            def at(self, p, k):
                return p * self.per + k

        class Bank:

            def __init__(self, name, tensor, uses):
                self.t = tensor
                self.before, fills, reads = {}, 0, 0
                self.first = uses[0][0]
                for use, f, r in uses:
                    self.before[use] = (fills, reads, f, r)
                    fills, reads = fills + f, reads + r
                self.filled, self.emptied = Count(name + "_filled", fills), Count(name + "_emptied", reads)

            def full(self, p, use):
                fills, _, f, _ = self.before[use]
                return self.filled.at(p, fills + f)

            def free(self, p, use):
                return self.emptied.at(p, self.before[use][1])

            def read(self, p, use):
                _, reads, _, r = self.before[use]
                return self.emptied.at(p, reads + r)

        def psum(name):
            return ctx.enter_context(nc.psum_tensor(name, [128, 512], F32))

        w = {}
        for name, shape in W_SHAPES.items():
            if name not in W_EARLY:
                w[name] = sb("w_" + name, list(shape))
        ws = {name: sb(f"ws_{name}", [128, 2, KC, columns], F32R) for name, columns in SPLIT.items()}
        bn_scale, bn_shift = sb("bn_scale", [128, 4]), sb("bn_shift", [128, 4])
        bn_v, bn_half = sb("bn_v", [128, 4]), sb("bn_half", [128, 4])
        bn_y, bn_t = sb("bn_y", [128, 4]), sb("bn_t", [128, 4])
        kvb1 = w["kvb1"]
        qb2s = sb("qb2s", [128, KC])
        pb2 = sb("pb2", [128, KC])
        qu3 = sb("qu3", [128, KC])
        ob3 = sb("ob3", [128, KC])
        bqk3 = sb("bqk3", [HALF, 1])

        x_in = sb("x_in", [128, KC, N2])
        with ExitStack() as early:
            for name in W_EARLY:
                w[name] = early.enter_context(nc.sbuf_tensor("w_" + name, list(W_SHAPES[name]), F32))
        x_res = sb("x_res", [128, KC, N2])
        xpad = sb("xpad", [128, KC, 2 * PAD, PAD])
        CR = 2 * PAD - 2
        y1 = sb("y1", [128, KC, 2 * PAD, SIDE])
        rs_d = sb("rs_d", [128, 2 * SIDE, 6])
        rs_x = sb("rs_x", [128, 2 * SIDE, R7])
        rs_e = sb("rs_e", [128, 2, 6, R7])
        yr = sb("yr", [128, KC, 2, 2, 64])
        q0 = sb("q0", [128, 2, N2])
        k0 = sb("k0", [128, 2, 2, T7])
        v0 = sb("v0", [128, 2, 2, 128])
        s0 = sb("s0", [HALF, 2, 8, T7])
        m0 = sb("m0", [HALF, 2, 8])
        d0 = sb("d0", [HALF, 2, 8])
        r0 = sb("r0", [HALF, 2, 8])
        p0 = sb("p0", [HALF, 8, 2, 64])
        pt0 = sb("pt0", [128, 2, 2, TOK])
        opad = sb("opad", [128, 2, 2 * PAD, PAD])
        y2 = sb("y2", [128, KC, 2 * PAD, SIDE])
        act0 = sb("act0", [128, KC, N2])
        x1 = sb("x1", [128, KC, N2])
        xn1 = sb("xn1", [128, KC, N2])
        xs1 = sb("xs1", [128, 2, KC, N2], F32R)
        kv = sb("kv", [HALF, 4, 2 * CH])
        nmk = sb("nmk", [HALF, 4])
        sk = sb("sk", [HALF, 4])
        rk = sb("rk", [HALF, 4])
        nmq = sb("nmq", [128, KC, 2])
        bq_less = sb("bq_less", [128, KC, 2])
        qe = sb("qe", [128, KC, N2])
        sq = sb("sq", [128, KC, 2])
        rq = sb("rq", [128, KC, 2])
        cx = sb("cx", [128, 2, KC, CH])
        x2 = sb("x2", [128, KC, N2])
        x2b = sb("x2b", [128, KC, N2])
        xn2 = sb("xn2", [128, KC, N2])
        xs2 = sb("xs2", [128, 2, KC, N2], F32R)
        q2 = sb("q2", [128, KC, N2])
        k2 = sb("k2", [128, KC, N2])
        v2 = sb("v2", [HALF, 2, 2, CH])
        nm2 = sb("nm2", [HALF, 2, 2])
        e2 = sb("e2", [HALF, 2, 2, TOK])
        den2 = sb("den2", [HALF, 4, H2])
        pt2 = sb("pt2", [HALF, 2, 2, TOK])
        a2 = sb("a2", [128, 2, KC, TOK])
        rden2 = sb("rden2", [HALF, 4, H2])
        rt2 = sb("rt2", [H2, 2 * TOK])
        x3 = sb("x3", [128, KC, N2])
        xn3 = sb("xn3", [128, KC, N2])
        xs3 = sb("xs3", [128, 2, KC, N2], F32R)
        v3t = sb("v3t", [HALF, 4, CH + 1])
        rb3 = sb("rb3", [HALF, 4])
        qt3 = sb("qt3", [128, KC, N2])
        m3 = sb("m3", [HALF, 4])
        t3 = sb("t3", [HALF, 4])
        rs3 = sb("rs3", [HALF, 4])
        nm3 = sb("nm3", [HALF, 4])
        e3 = sb("e3", [HALF, 4, TOK])
        s3 = sb("s3", [HALF, 4])
        r3 = sb("r3", [HALF, 4])
        pt3 = qt3[0:HALF].rearrange("p c (i n) -> p c i n", i=2)
        out = sb("out", [128, KC, N2])

        class GroupNorm:

            def __init__(self, n):
                self.stats = sb(f"gn{n}_stats", [128, 4, 6])
                self.mine = sb(f"gn{n}_mine", [128, 2, 4])
                self.sq = sb(f"gn{n}_sq", [128, 4])
                self.group = sb(f"gn{n}_group", [128, 2, 4])
                self.v = sb(f"gn{n}_v", [128, 4])
                self.half = sb(f"gn{n}_half", [128, 4])
                self.y = sb(f"gn{n}_y", [128, 4])
                self.t = sb(f"gn{n}_t", [128, 4])
                self.scale = sb(f"gn{n}_scale", [128, 4])
                self.shift = sb(f"gn{n}_shift", [128, 4])
                self.stat_steps = Count(f"gn{n}_stat_steps", 9)
                self.stats_ready = Count(f"gn{n}_stats_ready", 1)
                self.steps = Count(f"gn{n}_steps", 5 + 4 * NEWTON + 3)
                self.done = Count(f"gn{n}_done", 4)
                self.high = Count(f"gn{n}_high", KC)
                self.low = Count(f"gn{n}_low", KC)

        gn = {1: GroupNorm(1), 2: GroupNorm(2), 3: GroupNorm(3)}

        def uses(*names, reads=1):
            return [(name, 1, reads) for name in names]

        ps_b = psum("ps_b")
        bank_a = Bank("l0_attention", psum("ps_a"), [
            *uses("q0", "q1", "k"), *uses("v", reads=2), *uses("s0", "s1", "t0", "t1"), *uses("o0", "o1", reads=2)])
        bank_b = Bank("l0_tail", ps_b, uses("pw0", "pw1", "mlp0", "mlp1"))
        bank_n = Bank("l2_tail", ps_b, uses("rt", "rep0", "rep1", "proj0", "proj1"))
        bank_c = Bank("l1_main", psum("ps_c"), [
            *uses("gn", "kv0", "kv1", "kv2", "kv3"), *uses("q0", "q1", "ctx0", "ctx1", reads=2), *uses("out0", "out1")])
        bank_d = Bank("l2_head", psum("ps_d"), uses("gn", "q0", "k0", "v0", "q1", "k1", "v1"))
        bank_e = Bank("l3_main", psum("ps_e"), [
            *uses("gn", "v0", "v1", "v2", "v3", "q0", "q1"), *uses("s0", "s1", reads=2), *uses("t0", "t1"),
            *uses("o0", "o1", reads=2)])
        bank_s = Bank("l2_scores", psum("ps_s"), uses(*range(UNITS), reads=2))
        bank_t = Bank("l2_turned", psum("ps_t"), uses(*range(UNITS)))
        bank_o = Bank("l2_heads_out", psum("ps_o"), [(0, H2, 1), (1, H2, 1)])

        weights_in = sem("weights_in")
        consts_set = sem("consts_set")
        sp_held, pool_held, dve_held = sem("sp_held"), sem("pool_held"), sem("dve_held")
        bn_steps = sem("bn_steps")
        fold_filled = sem("fold_filled")
        early_high, early_steps = sem("early_high"), sem("early_steps")
        x_loaded = Count("x_loaded", 16)
        res_loaded = Count("res_loaded", 16)
        bn1_done = Count("bn1_done", KC)
        conv1_steps = Count("conv1_steps", KC * 9)
        resize_steps = Count("resize_steps", KC * 9)
        l0_soft_steps = Count("l0_soft_steps", 2 * 4)
        l0_exp_done = Count("l0_exp_done", 2)
        l0_probs = Count("l0_probs", 2)
        conv2_steps = Count("conv2_steps", KC * 9)
        act0_done = Count("act0_done", KC)
        k_less = Count("k_less", 4)
        k_exp_done = Count("k_exp_done", 4)
        k_rsum = Count("k_rsum", 4)
        k_scaled = Count("k_scaled", 4)
        q_less_steps = Count("q_less_steps", KC * 2)
        q_rsum = Count("q_rsum", KC)
        hop_done, out_ready = Count("hop_done", 16), Count("out_ready", 16)
        max2_done = Count("max2_done", UNITS)
        rden_done = Count("rden_done", 1)
        l3_less_steps = Count("l3_less_steps", 2 * 3)
        r_ready = Count("r_ready", 2)
        l3_rsum = Count("l3_rsum", 2)
        p3_done = Count("p3_done", 4)
        stored = Count("stored", 16)
        block = ctx.enter_context(nc.Block())

        splits = ((1, GN1, bank_c, xn1, xs1), (2, GN2, bank_d, xn2, xs2), (3, GN3, bank_e, xn3, xs3))

        def run(eng, step):
            for t in range(-1, LAST_LAG + 1):
                step(t)
            with eng.Fori(LAST_LAG + 1, PAIRS - 1) as t:
                step(t)
            for t in range(PAIRS - 1, PAIRS + LAST_LAG):
                step(t)

        def pair_of(t, u, start):
            if start % SLOTS != u:
                return None
            p = t - start // SLOTS
            return p if not isinstance(t, int) or 0 <= p < PAIRS else None

        def linker(eng, count, p, k):
            done = [k]

            def link(ins):
                done[0] += 1
                ins.then_inc(count.sem, 1)
                eng.wait_ge(count.sem, count.at(p, done[0]))
            return link

        def has_before(p):
            return not isinstance(p, int) or p > 0

        def of_image(i):
            return slice(i * TOK, (i + 1) * TOK)

        def of_tile(i, tc):
            return slice(i * TOK + tc * HALF, i * TOK + (tc + 1) * HALF)

        def of_chunk(m):
            return slice(128 * m, 128 * (m + 1))

        def conv_images(tile, c):
            return tile[:, c].rearrange("p (i r) n -> p i r n", i=2)[:, :, 0:SIDE, :]

        def inside(tile, c):
            return tile[:, c].rearrange("p (i r) n -> p i r n", i=2)[:, :, 1:SIDE + 1, 1:SIDE + 1]

        def window(tile, c, k):
            return tile[:, c, k // 3:k // 3 + CR, k % 3:k % 3 + SIDE]

        def turned(n):
            return pt2[:, n % 2].rearrange("p c n -> p (c n)")

        def of_fold(k):
            return slice(k * CH, (k + 1) * CH)

        def early_sources():
            def parts(name, k, src, at=0):
                columns = slice(at, at + src.shape[-1])
                return ws[name][:, 0, k, columns], ws[name][:, 1, k, columns], src
            for k in range(KC):
                yield parts("kv1", k, w["k1"][:, k])
                for name in ("q1", "q2", "k2", "v2"):
                    yield parts(name, k, w[name][:, k])
            for k in range(KC):
                yield parts("kv1", k, bank_a.t[:, of_fold(k)], CH)
                yield parts("q3", k, bank_c.t[:, of_fold(k)])
                yield parts("v3", k, (bank_d, bank_e)[k].t[:, 0:CH + 2])

        WEIGHTS = 16 * len(W_SHAPES)
        CONSTS = 5
        BN_STEPS = 3 + 3 * NEWTON + 3 + 1
        FOLDS = 6
        PLAIN = KC * 5
        FOLDED = KC * 3
        EARLY_STEPS = PLAIN + FOLDED + 5

        @block.sync
        def _(sp):
            for name in W_SHAPES:
                dst = w[name][:]
                if name in W_PARTS:
                    dst = dst[..., 0:W_PARTS[name]]
                sp.dma_start(dst, a[name]).then_inc(weights_in, 16)
            sp.wait_ge(weights_in, WEIGHTS)

            def alone():
                sp.sem_inc(sp_held, 1)

            def step(t):
                for u in range(SLOTS):
                    p = pair_of(t, u, LOAD_X)
                    if p is not None:
                        sp.wait_ge(bn1_done.sem, bn1_done.at(p, 0))
                        alone()
                        sp.dma_start(x_in[:].rearrange("p c n -> p (c n)"),
                                     a["x"][bass.ds(p, 1)].rearrange("o p n -> (o p) n")).then_inc(x_loaded.sem, 16)
                    p = pair_of(t, u, LOAD_RES)
                    if p is not None:
                        sp.wait_ge(bank_b.emptied.sem, bank_b.free(p, "pw0"))
                        alone()
                        sp.dma_start(x_res[:].rearrange("p c n -> p (c n)"),
                                     a["x"][bass.ds(p, 1)].rearrange("o p n -> (o p) n")).then_inc(res_loaded.sem, 16)
                    p = pair_of(t, u, HOP)
                    if p is not None:
                        sp.wait_ge(bank_c.emptied.sem, bank_c.read(p, "out1"))
                        alone()
                        if has_before(p):
                            sp.wait_ge(bank_n.emptied.sem, bank_n.read(p - 1, "proj1"))
                            alone()
                        sp.dma_start(x2b[:], x2[:]).then_inc(hop_done.sem, 16)
                    p = pair_of(t, u, HOP_OUT)
                    if p is not None:
                        sp.wait_ge(bank_n.emptied.sem, bank_n.read(p, "proj1"))
                        alone()
                        sp.wait_ge(stored.sem, stored.at(p, 0))
                        alone()
                        sp.dma_start(out[:], x3[:]).then_inc(out_ready.sem, 16)
                    p = pair_of(t, u, STORE)
                    if p is not None:
                        sp.wait_ge(bank_e.emptied.sem, bank_e.read(p, "o1"))
                        alone()
                        sp.dma_start(a["out"][bass.ds(p, 1)].rearrange("o p n -> (o p) n"),
                                     out[:].rearrange("p c n -> p (c n)")).then_inc(stored.sem, 16)
            run(sp, step)
            sp.wait_ge(stored.sem, stored.at(PAIRS, 0))

        @block.gpsimd
        def _(pool):
            g = nc.gpsimd
            pool.wait_ge(early_steps, EARLY_STEPS)
            for tile in (xpad, opad, yr, p0, v0):
                g.memset(tile[:], 0.0).then_inc(consts_set, 1)
            pool.wait_ge(consts_set, CONSTS)

            def alone():
                pool.sem_inc(pool_held, 1)

            def resize(p, c):
                link = linker(pool, resize_steps, p, 9 * c)
                pool.wait_ge(conv1_steps.sem, conv1_steps.at(p, KC * 8 + c + 1))
                y = conv_images(y1, c)
                d = rs_d[:].rearrange("p (i r) n -> p i r n", i=2)
                x = rs_x[:].rearrange("p (i r) n -> p i r n", i=2)
                frac_x = w["frac"][:].unsqueeze(1).broadcast_to([128, 2 * SIDE, 6])
                frac_y = w["frac"][:].unsqueeze(1).unsqueeze(3).broadcast_to([128, 2, 6, R7])
                link(g.tensor_tensor(d, y[:, :, :, 1:12:2], y[:, :, :, 0:11:2], ALU.subtract))
                link(g.tensor_tensor(rs_d[:], rs_d[:], frac_x, ALU.mult))
                link(g.tensor_tensor(x[:, :, :, 0:6], y[:, :, :, 0:11:2], d, ALU.add))
                alone()
                link(g.tensor_copy(x[:, :, :, 6], y[:, :, :, 13]))
                link(g.tensor_tensor(rs_e[:], x[:, :, 1:12:2, :], x[:, :, 0:11:2, :], ALU.subtract))
                link(g.tensor_tensor(rs_e[:], rs_e[:], frac_y, ALU.mult))
                if has_before(p):
                    pool.wait_ge(bank_a.emptied.sem, bank_a.read(p - 1, "v"))
                first = yr[:, c, :, 0, 0:T7].rearrange("p i (a b) -> p i a b", a=R7)
                link(g.tensor_tensor(first[:, :, 0:6, :], x[:, :, 0:11:2, :], rs_e[:], ALU.add))
                alone()
                link(g.tensor_copy(first[:, :, 6, :], x[:, :, 13, :]))
                alone()
                link(g.tensor_copy(yr[:, c, :, 1, 0:T7], yr[:, c, :, 0, 0:T7]))

            def normalized(p, n, bank, src, dst):
                t = gn[n]
                weight, bias = w[f"gn{n}_w"], w[f"gn{n}_b"]
                link = linker(pool, t.steps, p, 0)
                pool.wait_ge(bank.emptied.sem, bank.read(p, "gn"))
                pool.wait_ge(t.done.sem, t.done.at(p, 0))
                link(g.tensor_tensor(t.t[:], t.group[:, 0], t.group[:, 0], ALU.mult))
                link(g.tensor_tensor(t.v[:], t.group[:, 1], t.t[:], ALU.subtract))
                alone()
                link(g.tensor_scalar(t.v[:], t.v[:], 0.0, EPS, ALU.max, ALU.add))
                alone()
                link(g.tensor_scalar(t.half[:], t.v[:], -0.5, None, ALU.mult))
                alone()
                link(g.tensor_scalar(t.y[:].bitcast(I32), t.v[:].bitcast(I32), -0.5, MAGIC, ALU.mult, ALU.add))
                for _ in range(NEWTON):
                    link(g.tensor_tensor(t.t[:], t.y[:], t.y[:], ALU.mult))
                    link(g.tensor_tensor(t.t[:], t.t[:], t.half[:], ALU.mult))
                    alone()
                    link(g.tensor_scalar(t.t[:], t.t[:], 1.5, None, ALU.add))
                    link(g.tensor_tensor(t.y[:], t.y[:], t.t[:], ALU.mult))
                link(g.tensor_tensor(t.scale[:], t.y[:], weight[:], ALU.mult))
                link(g.tensor_tensor(t.t[:], t.group[:, 0], t.scale[:], ALU.mult))
                link(g.tensor_tensor(t.shift[:], bias[:], t.t[:], ALU.subtract))
                for c in range(KC):
                    for i in range(2):
                        j = 2 * c + i
                        alone()
                        g.tensor_scalar(dst[:, c, of_image(i)], src[:, c, of_image(i)], t.scale[:, j:j + 1],
                                        t.shift[:, j:j + 1], ALU.mult, ALU.add).then_inc(t.done.sem, 1)

            def step(t):
                for u in range(SLOTS):
                    for i in range(2):
                        p = pair_of(t, u, L0_SUM[i])
                        if p is not None:
                            pool.wait_ge(l0_soft_steps.sem, l0_soft_steps.at(p, 4 * (i + 1)))
                            pool.wait_ge(bank_a.emptied.sem, bank_a.free(p, "q0"))
                            g.tensor_tensor(p0[:, :, i, 0:T7], s0[:, i], r0[:, i].unsqueeze(2).broadcast_to([HALF, 8, T7]),
                                            ALU.mult).then_inc(l0_probs.sem, 1)
                    for j in range(4):
                        p = pair_of(t, u, L1_KV[j] + 1)
                        if p is not None:
                            pool.wait_ge(k_rsum.sem, k_rsum.at(p, j + 1))
                            alone()
                            g.tensor_scalar(kv[:, j, 0:CH], kv[:, j, 0:CH], rk[:, j:j + 1], None, ALU.mult).then_inc(k_scaled.sem, 1)
                    p = pair_of(t, u, L3_Q[0])
                    if p is not None:
                        pool.wait_ge(bank_e.emptied.sem, bank_e.read(p, "v3"))
                        pool.wait_ge(l3_less_steps.sem, l3_less_steps.at(p, 0))
                        alone()
                        g.tensor_scalar(rb3[:], v3t[:, :, CH], bqk3[:, 0:1], None, ALU.add).then_inc(r_ready.sem, 1)
                        pool.wait_ge(r_ready.sem, r_ready.at(p, 1))
                        alone()
                        g.tensor_scalar(rs3[:], rb3[:], SCALE3, None, ALU.mult).then_inc(r_ready.sem, 1)
                    for i in range(2):
                        p = pair_of(t, u, L3_S[i] + 1)
                        if p is not None:
                            pool.wait_ge(l3_rsum.sem, l3_rsum.at(p, i + 1))
                            for tc in range(2):
                                j = 2 * i + tc
                                alone()
                                g.tensor_scalar(e3[:, j], e3[:, j], r3[:, j:j + 1], None, ALU.mult).then_inc(p3_done.sem, 1)
                    p = pair_of(t, u, GN1[2])
                    if p is not None:
                        pool.wait_ge(bank_c.emptied.sem, bank_c.free(p, "gn"))
                        normalized(p, 1, bank_c, x1, xn1)
                    p = pair_of(t, u, GN2[2])
                    if p is not None:
                        pool.wait_ge(gn[2].low.sem, gn[2].low.at(p, 0))
                        normalized(p, 2, bank_d, x2, xn2)
                    p = pair_of(t, u, GN3[2])
                    if p is not None:
                        pool.wait_ge(bank_e.emptied.sem, bank_e.free(p, "gn"))
                        normalized(p, 3, bank_e, x3, xn3)
                    for c in range(KC):
                        p = pair_of(t, u, RESIZE[c])
                        if p is not None:
                            resize(p, c)
            run(pool, step)

        @block.scalar
        def _(act):
            s = nc.scalar
            act.wait_ge(weights_in, WEIGHTS)
            for n, (high, low, src) in enumerate(early_sources()):
                if n == PLAIN:
                    act.wait_ge(fold_filled, FOLDS)
                s.copy(high, src).then_inc(early_high, 1)
            act.wait_ge(early_steps, EARLY_STEPS)
            act.wait_ge(bn_steps, BN_STEPS)
            act.wait_ge(consts_set, CONSTS)

            def step(t):
                for u in range(SLOTS):
                    for n in range(UNITS):
                        p = pair_of(t, u, ATT + n + 1)
                        if p is not None:
                            act.wait_ge(bank_t.filled.sem, bank_t.full(p, n))
                            if n > 1 or has_before(p):
                                act.wait_ge(bank_o.filled.sem, bank_o.filled.at(p, n - 1))
                            s.copy(turned(n), bank_t.t[0:HALF, 0:N2]).then_inc(bank_t.emptied.sem, 1)
                    for n in range(UNITS):
                        p = pair_of(t, u, ATT + n)
                        if p is not None:
                            i, h = n // H2, n % H2
                            act.wait_ge(max2_done.sem, max2_done.at(p, n + 1))
                            if n or has_before(p):
                                act.wait_ge(bank_t.filled.sem, bank_t.filled.at(p, n - 1))
                            if h == 0:
                                act.wait_ge(rden_done.sem, rden_done.at(p, 0))
                            for tc in range(2):
                                s.activation(e2[:, n % 2, tc], bank_s.t[0:HALF, of_image(tc)], ACT.Exp,
                                             bias=nm2[:, n % 2, tc:tc + 1], accum_out=den2[:, 2 * i + tc, h:h + 1]
                                             ).then_inc(bank_s.emptied.sem, 1)
                    for c in range(KC):
                        p = pair_of(t, u, BN1[c])
                        if p is not None:
                            act.wait_ge(x_loaded.sem, x_loaded.at(p, 16))
                            if has_before(p):
                                act.wait_ge(conv1_steps.sem, conv1_steps.at(p - 1, KC * 8 + c + 1))
                            s.activation(inside(xpad, c), x_in[:, c].rearrange("p (i r n) -> p i r n", i=2, r=SIDE),
                                         ACT.Identity, scale=bn_scale[:, c:c + 1], bias=bn_shift[:, c:c + 1]
                                         ).then_inc(bn1_done.sem, 1)
                    for c in range(KC):
                        p = pair_of(t, u, L0_Q[c])
                        if p is not None:
                            act.wait_ge(bank_a.filled.sem, bank_a.full(p, f"q{c}"))
                            s.copy(q0[:, c], bank_a.t[:, 0:N2]).then_inc(bank_a.emptied.sem, 1)
                    p = pair_of(t, u, L0_K)
                    if p is not None:
                        act.wait_ge(bank_a.filled.sem, bank_a.full(p, "k"))
                        s.copy(k0[:].rearrange("p m i n -> p (m i n)"), bank_a.t[:, 0:4 * T7]).then_inc(bank_a.emptied.sem, 1)
                    p = pair_of(t, u, L0_V)
                    if p is not None:
                        act.wait_ge(bank_a.filled.sem, bank_a.full(p, "v"))
                        src = bank_a.t[:].rearrange("p (i m d) -> p i m d", i=2, m=2)
                        for hl in range(2):
                            half = slice(64 * hl, 64 * hl + 64)
                            s.copy(v0[half, :, :, half], src[half, :, :, half]).then_inc(bank_a.emptied.sem, 1)
                    for i in range(2):
                        p = pair_of(t, u, L0_S[i])
                        if p is not None:
                            act.wait_ge(l0_soft_steps.sem, l0_soft_steps.at(p, 4 * i + 2))
                            s.activation(s0[:, i], s0[:, i], ACT.Exp, scale=SCALE0).then_inc(l0_exp_done.sem, 1)
                        p = pair_of(t, u, L0_T[i])
                        if p is not None:
                            act.wait_ge(bank_a.filled.sem, bank_a.full(p, f"t{i}"))
                            s.copy(pt0[:, i].rearrange("p m n -> p (m n)"), bank_a.t[:, 0:N2]).then_inc(bank_a.emptied.sem, 1)
                        p = pair_of(t, u, L0_O[i])
                        if p is not None:
                            act.wait_ge(bank_a.filled.sem, bank_a.full(p, f"o{i}"))
                            act.wait_ge(conv2_steps.sem, conv2_steps.at(p, 0))
                            for m in range(2):
                                s.copy(opad[:, m, i * PAD + 1:i * PAD + 1 + SIDE, 1:SIDE + 1],
                                       bank_a.t[:, of_image(m)].rearrange("p (r n) -> p r n", r=SIDE)
                                       ).then_inc(bank_a.emptied.sem, 1)
                    for c in range(KC):
                        p = pair_of(t, u, L0_PW[c])
                        if p is not None:
                            act.wait_ge(bank_b.emptied.sem, bank_b.read(p, f"pw{c}"))
                            s.activation(act0[:, c], x1[:, c], ACT.Relu, scale=bn_scale[:, 2 + c:3 + c],
                                         bias=bn_shift[:, 2 + c:3 + c]).then_inc(act0_done.sem, 1)
                    for j in range(4):
                        p = pair_of(t, u, L1_KV[j])
                        if p is not None:
                            act.wait_ge(k_less.sem, k_less.at(p, j + 1))
                            s.activation(kv[:, j, 0:CH], kv[:, j, 0:CH], ACT.Exp, bias=nmk[:, j:j + 1],
                                         accum_out=sk[:, j:j + 1]).then_inc(k_exp_done.sem, 1)
                    for c in range(KC):
                        p = pair_of(t, u, L1_Q[c])
                        if p is not None:
                            act.wait_ge(q_less_steps.sem, q_less_steps.at(p, 2 * (c + 1)))
                            for i in range(2):
                                s.activation(qe[:, c, of_image(i)], bank_c.t[:, of_image(i)], ACT.Exp,
                                             bias=bq_less[:, c, i:i + 1], accum_out=sq[:, c, i:i + 1]
                                             ).then_inc(bank_c.emptied.sem, 1)
                    for i in range(2):
                        p = pair_of(t, u, L1_CTX[i])
                        if p is not None:
                            act.wait_ge(bank_c.filled.sem, bank_c.full(p, f"ctx{i}"))
                            act.wait_ge(q_rsum.sem, q_rsum.at(p, KC))
                            for c in range(KC):
                                s.activation(cx[:, i, c], bank_c.t[:, c * CH:(c + 1) * CH], ACT.Copy,
                                             scale=rq[:, c, i:i + 1]).then_inc(bank_c.emptied.sem, 1)
                    for n, stage, bank, src, dst in splits:
                        p = pair_of(t, u, stage[3])
                        if p is not None:
                            act.wait_ge(bank.emptied.sem, bank.free(p, bank.first))
                            for c in range(KC):
                                act.wait_ge(gn[n].done.sem, gn[n].done.at(p, 2 * (c + 1)))
                                s.copy(dst[:, 0, c], src[:, c]).then_inc(gn[n].high.sem, 1)
                    for c in range(KC):
                        p = pair_of(t, u, L2_QK[c][0])
                        if p is not None:
                            act.wait_ge(bank_d.filled.sem, bank_d.full(p, f"q{c}"))
                            s.activation(q2[:, c], bank_d.t[:, 0:N2], ACT.Identity, bias=qb2s[:, c:c + 1], scale=SCALE2
                                         ).then_inc(bank_d.emptied.sem, 1)
                        p = pair_of(t, u, L2_QK[c][1])
                        if p is not None:
                            act.wait_ge(bank_d.filled.sem, bank_d.full(p, f"k{c}"))
                            s.activation(k2[:, c], bank_d.t[:, 0:N2], ACT.Identity, bias=w["kb2"][:, c:c + 1]
                                         ).then_inc(bank_d.emptied.sem, 1)
                    for i in range(2):
                        p = pair_of(t, u, L2_V[i])
                        if p is not None:
                            act.wait_ge(bank_d.filled.sem, bank_d.full(p, f"v{i}"))
                            s.copy(v2[:, i].rearrange("p c n -> p (c n)"), bank_d.t[0:HALF, :]).then_inc(bank_d.emptied.sem, 1)
                    for i in range(2):
                        p = pair_of(t, u, ATT + H2 * (i + 1) + 1)
                        if p is not None:
                            act.wait_ge(bank_o.filled.sem, bank_o.full(p, i))
                            act.wait_ge(bank_n.emptied.sem, bank_n.free(p, "rt"))
                            s.copy(a2[:, i].rearrange("p c n -> p (c n)"), bank_o.t[:, 0:N2]).then_inc(bank_o.emptied.sem, 1)
                    for j in range(4):
                        p = pair_of(t, u, L3_V[j])
                        if p is not None:
                            act.wait_ge(bank_e.filled.sem, bank_e.full(p, f"v{j}"))
                            s.copy(v3t[:, j], bank_e.t[0:HALF, 0:CH + 1]).then_inc(bank_e.emptied.sem, 1)
                    for c in range(KC):
                        p = pair_of(t, u, L3_Q[c])
                        if p is not None:
                            act.wait_ge(bank_e.filled.sem, bank_e.full(p, f"q{c}"))
                            s.activation(qt3[:, c], bank_e.t[:, 0:N2], ACT.Identity, bias=qu3[:, c:c + 1]
                                         ).then_inc(bank_e.emptied.sem, 1)
                    for i in range(2):
                        p = pair_of(t, u, L3_S[i])
                        if p is not None:
                            act.wait_ge(l3_less_steps.sem, l3_less_steps.at(p, 3 * (i + 1)))
                            for tc in range(2):
                                j = 2 * i + tc
                                s.activation(e3[:, j], bank_e.t[0:HALF, of_image(tc)], ACT.Exp, scale=SCALE3,
                                             bias=nm3[:, j:j + 1], accum_out=s3[:, j:j + 1]
                                             ).then_inc(bank_e.emptied.sem, 1)
                        p = pair_of(t, u, L3_T[i])
                        if p is not None:
                            act.wait_ge(bank_e.filled.sem, bank_e.full(p, f"t{i}"))
                            s.copy(pt3[:, i].rearrange("p c n -> p (c n)"), bank_e.t[0:HALF, 0:N2]
                                   ).then_inc(bank_e.emptied.sem, 1)
            run(act, step)

        @block.vector
        def _(dve):
            v = nc.vector

            def rsqrt(link, x, half, y, tmp):
                link(v.tensor_scalar(half, x, -0.5, None, ALU.mult))
                link(v.tensor_scalar(y.bitcast(I32), x.bitcast(I32), -0.5, MAGIC, ALU.mult, ALU.add))
                for _ in range(NEWTON):
                    link(v.tensor_tensor(tmp, y, y, ALU.mult))
                    link(v.tensor_tensor(tmp, tmp, half, ALU.mult))
                    link(v.scalar_tensor_tensor(out=y, in0=tmp, scalar=1.5, in1=y, op0=ALU.add, op1=ALU.mult))

            dve.wait_ge(weights_in, WEIGHTS)
            bn_done = [0]

            def bn_link(ins):
                bn_done[0] += 1
                ins.then_inc(bn_steps, 1)
                dve.wait_ge(bn_steps, bn_done[0])
            bn_link(v.tensor_scalar(bn_v[:], w["bn_v"][:], EPS, None, ALU.add))
            rsqrt(bn_link, bn_v[:], bn_half[:], bn_y[:], bn_t[:])
            bn_link(v.tensor_tensor(bn_scale[:], bn_y[:], w["bn_g"][:], ALU.mult))
            bn_link(v.tensor_tensor(bn_t[:], bn_scale[:], w["bn_m"][:], ALU.mult))
            bn_link(v.tensor_tensor(bn_shift[:], w["bn_b"][:], bn_t[:], ALU.subtract))
            bn_link(v.tensor_scalar(qb2s[:], w["qb2"][:], SCALE2, None, ALU.mult))
            assert bn_done[0] == BN_STEPS
            for n, (high, low, src) in enumerate(early_sources()):
                dve.wait_ge(early_high, n + 1 if n < PLAIN else PLAIN + FOLDED)
                v.tensor_tensor(low, src, high, ALU.subtract).then_inc(early_steps, 1)
            dve.wait_ge(fold_filled, FOLDS)
            v.tensor_copy(kvb1[:, CH:2 * CH], ps_b[0:HALF, 0:CH]).then_inc(early_steps, 1)
            v.tensor_tensor(pb2[:], bank_s.t[:, 0:KC], w["pb2"][:], ALU.add).then_inc(early_steps, 1)
            v.tensor_copy(qu3[:], bank_s.t[:, 2:2 + KC]).then_inc(early_steps, 1)
            v.tensor_tensor(ob3[:], bank_s.t[:, 4:4 + KC], w["ob3"][:], ALU.add).then_inc(early_steps, 1)
            v.tensor_copy(bqk3[:], bank_s.t[0:HALF, 6:7]).then_inc(early_steps, 1)
            dve.wait_ge(early_steps, EARLY_STEPS)

            def group_stats(p, n, src):
                t = gn[n]
                link = linker(dve, t.stat_steps, p, 8)
                dve.wait_ge(t.steps.sem, t.steps.at(p, 0))
                for j in range(4):
                    v.bn_stats(t.stats[:, j], src[:, j // 2, of_image(j % 2)]).then_inc(t.stat_steps.sem, 1)
                for j in range(4):
                    dve.wait_ge(t.stat_steps.sem, t.stat_steps.at(p, j + 1))
                    dve.sem_inc(dve_held, 1)
                    v.bn_aggr(t.mine[:, :, j], t.stats[:, j]).then_inc(t.stat_steps.sem, 1)
                dve.wait_ge(t.stat_steps.sem, t.stat_steps.at(p, 8))
                link(v.tensor_tensor(t.sq[:], t.mine[:, 0], t.mine[:, 0], ALU.mult))
                v.tensor_tensor(t.mine[:, 1], t.mine[:, 1], t.sq[:], ALU.add).then_inc(t.stats_ready.sem, 1)

            def group_means(p, n, bank):
                t = gn[n]
                dve.wait_ge(bank.filled.sem, bank.full(p, "gn"))
                dve.wait_ge(t.steps.sem, t.steps.at(p, 0))
                v.tensor_copy(t.group[:], bank.t[:, 0:8].rearrange("p (a b) -> p a b", a=2)).then_inc(bank.emptied.sem, 1)

            def step(t):
                for u in range(SLOTS):
                    for n in range(UNITS):
                        p = pair_of(t, u, ATT + n)
                        if p is not None:
                            dve.wait_ge(bank_s.filled.sem, bank_s.full(p, n))
                            v.tensor_reduce(out=nm2[:, n % 2], in_=bank_s.t[0:HALF, 0:N2].rearrange("p (c n) -> p c n", c=2),
                                            axis=AX.X, op=ALU.max, negate=True).then_inc(max2_done.sem, 1)
                    for i in range(2):
                        p = pair_of(t, u, L0_S[i])
                        if p is not None:
                            dve.wait_ge(bank_a.filled.sem, bank_a.full(p, f"s{i}"))
                            dve.wait_ge(l0_probs.sem, l0_probs.at(p, 0))
                            v.tensor_tensor(s0[:, i].rearrange("p (i j) n -> p i j n", i=2),
                                            bank_a.t[0:HALF, 0:8 * T7].rearrange("p (i j n) -> p i j n", i=2, j=4),
                                            w["bias0"][:, i].unsqueeze(1).broadcast_to([HALF, 2, 4, T7]),
                                            ALU.add).then_inc(bank_a.emptied.sem, 1)
                            dve.wait_ge(bank_a.emptied.sem, bank_a.read(p, f"s{i}"))
                            link = linker(dve, l0_soft_steps, p, 4 * i)
                            link(v.tensor_reduce(out=m0[:, i], in_=s0[:, i], axis=AX.X, op=ALU.max, negate=True))
                            v.tensor_tensor(s0[:, i], s0[:, i], m0[:, i].unsqueeze(2).broadcast_to([HALF, 8, T7]),
                                            ALU.add).then_inc(l0_soft_steps.sem, 1)
                        p = pair_of(t, u, L0_SUM[i])
                        if p is not None:
                            dve.wait_ge(l0_exp_done.sem, l0_exp_done.at(p, i + 1))
                            dve.wait_ge(l0_probs.sem, l0_probs.at(p, 0))
                            link = linker(dve, l0_soft_steps, p, 4 * i + 2)
                            link(v.tensor_reduce(out=d0[:, i], in_=s0[:, i], axis=AX.X, op=ALU.add))
                            v.reciprocal(r0[:, i], d0[:, i]).then_inc(l0_soft_steps.sem, 1)
                    for c in range(KC):
                        p = pair_of(t, u, L0_PW[c])
                        if p is not None:
                            dve.wait_ge(bank_b.filled.sem, bank_b.full(p, f"pw{c}"))
                            dve.wait_ge(res_loaded.sem, res_loaded.at(p, 16))
                            dve.wait_ge(gn[1].done.sem, gn[1].done.at(p, 0))
                            v.tensor_tensor(x1[:, c], bank_b.t[:, 0:N2], x_res[:, c], ALU.add
                                            ).then_inc(bank_b.emptied.sem, 1)
                        p = pair_of(t, u, L0_MLP[c])
                        if p is not None:
                            dve.wait_ge(bank_b.filled.sem, bank_b.full(p, f"mlp{c}"))
                            dve.wait_ge(act0_done.sem, act0_done.at(p, KC))
                            v.tensor_tensor(x1[:, c], bank_b.t[:, 0:N2], x1[:, c], ALU.add
                                            ).then_inc(bank_b.emptied.sem, 1)
                    p = pair_of(t, u, GN1[0])
                    if p is not None:
                        dve.wait_ge(bank_b.emptied.sem, bank_b.read(p, "mlp1"))
                        group_stats(p, 1, x1)
                    p = pair_of(t, u, GN1[1])
                    if p is not None:
                        group_means(p, 1, bank_c)
                    for j in range(4):
                        p = pair_of(t, u, L1_KV[j])
                        if p is not None:
                            dve.wait_ge(bank_c.filled.sem, bank_c.full(p, f"kv{j}"))
                            v.tensor_tensor(kv[:, j], bank_c.t[0:HALF, :], kvb1[:], ALU.add).then_inc(bank_c.emptied.sem, 1)
                            dve.wait_ge(bank_c.emptied.sem, bank_c.read(p, f"kv{j}"))
                            v.tensor_reduce(out=nmk[:, j:j + 1], in_=kv[:, j, 0:CH], axis=AX.X, op=ALU.max, negate=True
                                            ).then_inc(k_less.sem, 1)
                        p = pair_of(t, u, L1_KV[j] + 1)
                        if p is not None:
                            dve.wait_ge(k_exp_done.sem, k_exp_done.at(p, j + 1))
                            dve.wait_ge(k_scaled.sem, k_scaled.at(p, 0))
                            v.reciprocal(rk[:, j:j + 1], sk[:, j:j + 1]).then_inc(k_rsum.sem, 1)
                    for c in range(KC):
                        p = pair_of(t, u, L1_Q[c])
                        if p is not None:
                            dve.wait_ge(bank_c.filled.sem, bank_c.full(p, f"q{c}"))
                            link = linker(dve, q_less_steps, p, 2 * c)
                            link(v.tensor_reduce(out=nmq[:, c], in_=bank_c.t[:, 0:N2].rearrange("p (i n) -> p i n", i=2),
                                                 axis=AX.X, op=ALU.max, negate=True))
                            v.tensor_scalar(bq_less[:, c], nmq[:, c], w["qb1"][:, c:c + 1], w["qb1"][:, c:c + 1],
                                            ALU.subtract, ALU.add).then_inc(q_less_steps.sem, 1)
                        p = pair_of(t, u, L1_Q[c] + 1)
                        if p is not None:
                            dve.wait_ge(bank_c.emptied.sem, bank_c.read(p, f"q{c}"))
                            v.reciprocal(rq[:, c], sq[:, c]).then_inc(q_rsum.sem, 1)
                    for c in range(KC):
                        p = pair_of(t, u, L1_OUT[c])
                        if p is not None:
                            dve.wait_ge(bank_c.filled.sem, bank_c.full(p, f"out{c}"))
                            dve.wait_ge(gn[2].done.sem, gn[2].done.at(p, 0))
                            dve.wait_ge(hop_done.sem, hop_done.at(p, 0))
                            v.scalar_tensor_tensor(out=x2[:, c], in0=bank_c.t[:, 0:N2], scalar=w["pb1"][:, c:c + 1],
                                                   in1=xn1[:, c], op0=ALU.add, op1=ALU.add
                                                   ).then_inc(bank_c.emptied.sem, 1)
                    p = pair_of(t, u, L2_RDEN)
                    if p is not None:
                        dve.wait_ge(bank_s.emptied.sem, bank_s.read(p, UNITS - 1))
                        dve.wait_ge(bank_n.filled.sem, bank_n.filled.at(p, 0))
                        v.reciprocal(rden2[:], den2[:]).then_inc(rden_done.sem, 1)
                    p = pair_of(t, u, L2_RT)
                    if p is not None:
                        dve.wait_ge(bank_n.filled.sem, bank_n.full(p, "rt"))
                        v.tensor_copy(rt2[:], bank_n.t[0:H2, 0:N2]).then_inc(bank_n.emptied.sem, 1)
                    for i in range(2):
                        p = pair_of(t, u, L2_REP[i])
                        if p is not None:
                            dve.wait_ge(bank_n.filled.sem, bank_n.full(p, f"rep{i}"))
                            dve.wait_ge(bank_o.emptied.sem, bank_o.emptied.at(p, i + 1))
                            v.tensor_tensor(a2[:, i].rearrange("p c n -> p (c n)"), bank_n.t[:, 0:N2],
                                            a2[:, i].rearrange("p c n -> p (c n)"), ALU.mult
                                            ).then_inc(bank_n.emptied.sem, 1)
                    for c in range(KC):
                        p = pair_of(t, u, L2_PROJ[c])
                        if p is not None:
                            dve.wait_ge(bank_n.filled.sem, bank_n.full(p, f"proj{c}"))
                            dve.wait_ge(hop_done.sem, hop_done.at(p, 16))
                            dve.wait_ge(gn[3].done.sem, gn[3].done.at(p, 0))
                            dve.wait_ge(out_ready.sem, out_ready.at(p, 0))
                            v.scalar_tensor_tensor(out=x3[:, c], in0=bank_n.t[:, 0:N2], scalar=pb2[:, c:c + 1],
                                                   in1=x2b[:, c], op0=ALU.add, op1=ALU.add
                                                   ).then_inc(bank_n.emptied.sem, 1)
                    for n, stage, _, src, dst in splits:
                        p = pair_of(t, u, stage[3])
                        if p is not None:
                            for c in range(KC):
                                dve.wait_ge(gn[n].high.sem, gn[n].high.at(p, c + 1))
                                v.tensor_tensor(dst[:, 1, c], src[:, c], dst[:, 0, c], ALU.subtract).then_inc(gn[n].low.sem, 1)
                    p = pair_of(t, u, GN2[0])
                    if p is not None:
                        dve.wait_ge(bank_c.emptied.sem, bank_c.read(p, "out1"))
                        group_stats(p, 2, x2)
                    p = pair_of(t, u, GN2[1])
                    if p is not None:
                        group_means(p, 2, bank_d)
                    p = pair_of(t, u, GN3[0])
                    if p is not None:
                        dve.wait_ge(bank_n.emptied.sem, bank_n.read(p, "proj1"))
                        group_stats(p, 3, x3)
                    p = pair_of(t, u, GN3[1])
                    if p is not None:
                        group_means(p, 3, bank_e)
                    for i in range(2):
                        p = pair_of(t, u, L3_S[i])
                        if p is not None:
                            both = slice(2 * i, 2 * i + 2)
                            dve.wait_ge(bank_e.filled.sem, bank_e.full(p, f"s{i}"))
                            dve.wait_ge(r_ready.sem, r_ready.at(p, 2))
                            link = linker(dve, l3_less_steps, p, 3 * i)
                            link(v.tensor_reduce(out=m3[:, both], in_=bank_e.t[0:HALF, 0:N2].rearrange("p (c n) -> p c n", c=2),
                                                 axis=AX.X, op=ALU.max))
                            link(v.tensor_tensor(t3[:, both], m3[:, both], rb3[:, both], ALU.add))
                            v.scalar_tensor_tensor(out=nm3[:, both], in0=t3[:, both], scalar=-SCALE3, in1=rs3[:, both],
                                                   op0=ALU.mult, op1=ALU.add).then_inc(l3_less_steps.sem, 1)
                        p = pair_of(t, u, L3_S[i] + 1)
                        if p is not None:
                            dve.wait_ge(bank_e.emptied.sem, bank_e.read(p, f"s{i}"))
                            dve.wait_ge(p3_done.sem, p3_done.at(p, 0))
                            v.reciprocal(r3[:, 2 * i:2 * i + 2], s3[:, 2 * i:2 * i + 2]).then_inc(l3_rsum.sem, 1)
                    for i in range(2):
                        p = pair_of(t, u, L3_O[i])
                        if p is not None:
                            dve.wait_ge(bank_e.filled.sem, bank_e.full(p, f"o{i}"))
                            dve.wait_ge(out_ready.sem, out_ready.at(p, 16))
                            for m in range(KC):
                                v.scalar_tensor_tensor(out=out[:, m, of_image(i)], in0=bank_e.t[:, of_image(m)],
                                                       scalar=ob3[:, m:m + 1], in1=out[:, m, of_image(i)],
                                                       op0=ALU.add, op1=ALU.add).then_inc(bank_e.emptied.sem, 1)
                    for k in range(9):
                        p = pair_of(t, u, CONV1[k])
                        if p is not None:
                            for c in range(KC):
                                dst, tap = y1[:, c, 0:CR], w["dw1"][:, c, k:k + 1]
                                if k == 0:
                                    dve.wait_ge(bn1_done.sem, bn1_done.at(p, c + 1))
                                    if has_before(p):
                                        dve.wait_ge(bank_a.emptied.sem, bank_a.read(p - 1, "q1"))
                                        dve.wait_ge(resize_steps.sem, resize_steps.at(p, 0))
                                    v.tensor_scalar(dst, window(xpad, c, k), tap, None, ALU.mult).then_inc(conv1_steps.sem, 1)
                                else:
                                    dve.wait_ge(conv1_steps.sem, conv1_steps.at(p, KC * (k - 1) + c + 1))
                                    v.scalar_tensor_tensor(out=dst, in0=window(xpad, c, k), scalar=tap, in1=dst,
                                                           op0=ALU.mult, op1=ALU.add).then_inc(conv1_steps.sem, 1)
                    for k in range(9):
                        p = pair_of(t, u, CONV2[k])
                        if p is not None:
                            for c in range(KC):
                                dst, tap = y2[:, c, 0:CR], w["dw2"][:, c, k:k + 1]
                                if k == 0:
                                    dve.wait_ge(bank_a.emptied.sem, bank_a.read(p, "o1"))
                                    dve.wait_ge(bank_b.emptied.sem, bank_b.free(p, "pw0"))
                                    v.tensor_scalar(dst, window(opad, c, k), tap, None, ALU.mult).then_inc(conv2_steps.sem, 1)
                                else:
                                    dve.wait_ge(conv2_steps.sem, conv2_steps.at(p, KC * (k - 1) + c + 1))
                                    v.scalar_tensor_tensor(out=dst, in0=window(opad, c, k), scalar=tap, in1=dst,
                                                           op0=ALU.mult, op1=ALU.add).then_inc(conv2_steps.sem, 1)
            run(dve, step)

        @block.tensor
        def _(pe):
            def mm(dst, lhsT, rhs, start, stop):
                return nc.tensor.matmul(dst, lhsT, rhs, start=start, stop=stop)

            def product(dst, lhsT, rhs, ks=KC):
                for k in range(ks):
                    ins = mm(dst, lhsT(k), rhs(k), k == 0, k == ks - 1)
                return ins

            def split_product(dst, lhsT, rhs):
                terms = [(k, a, b) for k in range(KC) for a, b in ((0, 0), (0, 1), (1, 0))]
                for k, a, b in terms:
                    ins = mm(dst, lhsT(a, k), rhs(b, k), (k, a, b) == terms[0], (k, a, b) == terms[-1])
                return ins

            eye = w["eye"]
            pe.wait_ge(weights_in, WEIGHTS)
            for m in range(KC):
                last = product(bank_a.t[:, m * CH:(m + 1) * CH], lambda k: w["v1"][:, k, of_chunk(m)], lambda k: w["p1"][:, k])
            last.then_inc(fold_filled, 1)
            product(ps_b[0:HALF, 0:CH], lambda k: w["vb1_rep"][:, k], lambda k: w["p1"][:, k]).then_inc(fold_filled, 1)
            for m in range(KC):
                last = product(bank_c.t[:, m * CH:(m + 1) * CH], lambda k: w["q3"][:, k, of_chunk(m)], lambda k: w["k3"][:, k])
            last.then_inc(fold_filled, 1)
            for m, t in enumerate((bank_d.t, bank_e.t)):
                product(t[:, 0:CH], lambda k: w["v3"][:, k, of_chunk(m)], lambda k: w["o3"][:, k])
                product(t[:, CH:CH + 2], lambda k: w["q3"][:, k, of_chunk(m)],
                        lambda k: w["kb3"][:, k:k + 1].broadcast_to([128, 2])).then_inc(fold_filled, 1)
            for m in range(KC):
                product(bank_s.t[:, m:m + 1], lambda k: w["p2"][:, k, of_chunk(m)], lambda k: w["vb2"][:, k:k + 1])
                product(bank_s.t[:, 2 + m:3 + m], lambda k: w["k3"][:, k, of_chunk(m)], lambda k: w["qb3"][:, k:k + 1])
                product(bank_s.t[:, 4 + m:5 + m], lambda k: w["o3"][:, k, of_chunk(m)], lambda k: w["vb3"][:, k:k + 1])
            product(bank_s.t[0:HALF, 6:7], lambda k: w["qb3_rep"][:, k], lambda k: w["kb3"][:, k:k + 1]).then_inc(fold_filled, 1)
            pe.wait_ge(early_steps, EARLY_STEPS)
            pe.wait_ge(consts_set, CONSTS)

            def scores2(p, n):
                i, c, r = n // H2, (n % H2) // 4, 32 * (n % 4)
                pe.wait_ge(bank_s.emptied.sem, bank_s.free(p, n))
                if n == 0:
                    pe.wait_ge(bank_d.emptied.sem, bank_d.read(p, "k0"))
                if n == 4:
                    pe.wait_ge(bank_d.emptied.sem, bank_d.read(p, "k1"))
                for tc in range(2):
                    last = mm(bank_s.t[0:HALF, of_image(tc)], q2[r:r + 32, c, of_tile(i, tc)],
                              k2[r:r + 32, c, of_image(i)], True, True)
                last.then_inc(bank_s.filled.sem, 1)

            def turn2(p, n):
                pe.wait_ge(bank_t.emptied.sem, bank_t.free(p, n))
                pe.wait_ge(bank_s.emptied.sem, bank_s.read(p, n))
                for tc in range(2):
                    for sc in range(2):
                        last = nc.tensor.transpose(bank_t.t[0:HALF, of_tile(sc, tc)],
                                                   e2[:, n % 2, tc, sc * HALF:(sc + 1) * HALF], eye[0:HALF, 0:HALF])
                last.then_inc(bank_t.filled.sem, 1)

            def values2(p, n):
                i, h = n // H2, n % H2
                c, r = h // 4, 32 * (h % 4)
                if h == 0:
                    pe.wait_ge(bank_o.emptied.sem, bank_o.free(p, i))
                    pe.wait_ge(bank_d.emptied.sem, bank_d.read(p, f"v{i}"))
                pe.wait_ge(bank_t.emptied.sem, bank_t.read(p, n))
                product(bank_o.t[r:r + 32, of_image(c)], lambda sc: v2[:, i, sc, 32 * h:32 * h + 32],
                        lambda sc: pt2[:, n % 2, sc]).then_inc(bank_o.filled.sem, 1)

            def step(t):
                for u in range(SLOTS):
                    for n in range(UNITS):
                        p = pair_of(t, u, ATT + n + 1)
                        if p is not None:
                            turn2(p, n)
                    for n in range(UNITS):
                        p = pair_of(t, u, ATT + n)
                        if p is not None:
                            scores2(p, n)
                    for c in range(KC):
                        p = pair_of(t, u, L0_Q[c])
                        if p is not None:
                            pe.wait_ge(bank_a.emptied.sem, bank_a.free(p, f"q{c}"))
                            pe.wait_ge(conv1_steps.sem, conv1_steps.at(p, KC * 9))
                            product(bank_a.t[:, 0:N2], lambda k: w["q0"][:, k, of_chunk(c)],
                                    lambda k: y1[:, k].rearrange("p (i r) n -> p i (r n)", i=2)[:, :, 0:TOK]
                                    ).then_inc(bank_a.filled.sem, 1)
                    p = pair_of(t, u, L0_K)
                    if p is not None:
                        pe.wait_ge(bank_a.emptied.sem, bank_a.free(p, "k"))
                        pe.wait_ge(resize_steps.sem, resize_steps.at(p, 9 * KC))
                        for m in range(2):
                            last = product(bank_a.t[:, 2 * T7 * m:2 * T7 * (m + 1)], lambda k: w["k0"][:, k, of_chunk(m)],
                                           lambda k: yr[:, k, :, 0, 0:T7])
                        last.then_inc(bank_a.filled.sem, 1)
                    p = pair_of(t, u, L0_V)
                    if p is not None:
                        pe.wait_ge(bank_a.emptied.sem, bank_a.free(p, "v"))
                        for i in range(2):
                            last = product(bank_a.t[:, i * CH:(i + 1) * CH],
                                           lambda k: yr[:, k, i].rearrange("p a n -> p (a n)"), lambda k: w["v0"][:, k])
                        last.then_inc(bank_a.filled.sem, 1)
                    for i in range(2):
                        p = pair_of(t, u, L0_S[i])
                        if p is not None:
                            pe.wait_ge(bank_a.emptied.sem, bank_a.free(p, f"s{i}"))
                            r = 64 * i
                            for j in range(8):
                                image, tc, m = j // 4, j // 2 % 2, j % 2
                                last = mm(bank_a.t[0:HALF, j * T7:(j + 1) * T7], q0[r:r + 64, m, of_tile(image, tc)],
                                          k0[r:r + 64, m, image], True, True)
                            last.then_inc(bank_a.filled.sem, 1)
                        p = pair_of(t, u, L0_T[i])
                        if p is not None:
                            pe.wait_ge(bank_a.emptied.sem, bank_a.free(p, f"t{i}"))
                            pe.wait_ge(l0_probs.sem, l0_probs.at(p, 2))
                            for tc in range(2):
                                for m in range(2):
                                    last = nc.tensor.transpose(bank_a.t[:, of_tile(m, tc)],
                                                               p0[:, 4 * i + 2 * tc + m].rearrange("p h n -> p (h n)"),
                                                               eye[0:HALF, 0:HALF])
                            last.then_inc(bank_a.filled.sem, 1)
                        p = pair_of(t, u, L0_O[i])
                        if p is not None:
                            pe.wait_ge(bank_a.emptied.sem, bank_a.free(p, f"o{i}"))
                            for m in range(2):
                                last = mm(bank_a.t[:, of_image(m)], v0[:, i, m], pt0[:, i, m], True, True)
                            last.then_inc(bank_a.filled.sem, 1)
                    for c in range(KC):
                        p = pair_of(t, u, L0_PW[c])
                        if p is not None:
                            if c == 0 and not (isinstance(p, int) and p < 3):
                                pe.wait_ge(bank_n.emptied.sem, bank_n.free(p - 2, "rt"))
                            pe.wait_ge(bank_b.emptied.sem, bank_b.free(p, f"pw{c}"))
                            pe.wait_ge(conv2_steps.sem, conv2_steps.at(p, KC * 9))
                            product(bank_b.t[:, 0:N2], lambda k: w["o0"][:, k, of_chunk(c)],
                                    lambda k: y2[:, k].rearrange("p (i r) n -> p i (r n)", i=2)[:, :, 0:TOK]
                                    ).then_inc(bank_b.filled.sem, 1)
                        p = pair_of(t, u, L0_MLP[c])
                        if p is not None:
                            pe.wait_ge(bank_b.emptied.sem, bank_b.free(p, f"mlp{c}"))
                            pe.wait_ge(act0_done.sem, act0_done.at(p, KC))
                            product(bank_b.t[:, 0:N2], lambda k: w["mlp0"][:, k, of_chunk(c)],
                                    lambda k: act0[:, k]).then_inc(bank_b.filled.sem, 1)
                    for j in range(4):
                        p = pair_of(t, u, L1_KV[j])
                        if p is not None:
                            pe.wait_ge(bank_c.emptied.sem, bank_c.free(p, f"kv{j}"))
                            pe.wait_ge(gn[1].low.sem, gn[1].low.at(p, KC))
                            split_product(bank_c.t[0:HALF, :], lambda a, k: xs1[:, a, k, of_tile(j // 2, j % 2)],
                                          lambda b, k: ws["kv1"][:, b, k]).then_inc(bank_c.filled.sem, 1)
                    for c in range(KC):
                        p = pair_of(t, u, L1_Q[c])
                        if p is not None:
                            pe.wait_ge(bank_c.emptied.sem, bank_c.free(p, f"q{c}"))
                            split_product(bank_c.t[:, 0:N2], lambda a, k: ws["q1"][:, a, k, of_chunk(c)],
                                          lambda b, k: xs1[:, b, k]).then_inc(bank_c.filled.sem, 1)
                    for i in range(2):
                        p = pair_of(t, u, L1_CTX[i])
                        if p is not None:
                            pe.wait_ge(bank_c.emptied.sem, bank_c.free(p, f"ctx{i}"))
                            pe.wait_ge(k_scaled.sem, k_scaled.at(p, 2 * (i + 1)))
                            for c in range(KC):
                                last = product(bank_c.t[:, c * CH:(c + 1) * CH], lambda k: kv[:, 2 * i + k, of_chunk(c)],
                                               lambda k: kv[:, 2 * i + k, CH:2 * CH])
                            last.then_inc(bank_c.filled.sem, 1)
                    for c in range(KC):
                        p = pair_of(t, u, L1_OUT[c])
                        if p is not None:
                            pe.wait_ge(bank_c.emptied.sem, bank_c.free(p, f"out{c}"))
                            for i in range(2):
                                last = product(bank_c.t[:, of_image(i)], lambda k: cx[:, i, k, of_chunk(c)],
                                               lambda k: qe[:, k, of_image(i)])
                            last.then_inc(bank_c.filled.sem, 1)
                    for c in range(KC):
                        for name, start in zip(("q", "k"), L2_QK[c]):
                            p = pair_of(t, u, start)
                            if p is not None:
                                pe.wait_ge(bank_d.emptied.sem, bank_d.free(p, f"{name}{c}"))
                                pe.wait_ge(gn[2].low.sem, gn[2].low.at(p, KC))
                                split_product(bank_d.t[:, 0:N2], lambda a, k: ws[f"{name}2"][:, a, k, of_chunk(c)],
                                              lambda b, k: xs2[:, b, k]).then_inc(bank_d.filled.sem, 1)
                    for i in range(2):
                        p = pair_of(t, u, L2_V[i])
                        if p is not None:
                            pe.wait_ge(bank_d.emptied.sem, bank_d.free(p, f"v{i}"))
                            for tc in range(2):
                                last = split_product(bank_d.t[0:HALF, tc * CH:(tc + 1) * CH],
                                                     lambda a, k: xs2[:, a, k, of_tile(i, tc)],
                                                     lambda b, k: ws["v2"][:, b, k])
                            last.then_inc(bank_d.filled.sem, 1)
                    for n, stage, bank, group in ((1, GN1, bank_c, "group32"), (2, GN2, bank_d, "group8"),
                                                  (3, GN3, bank_e, "group8")):
                        p = pair_of(t, u, stage[1])
                        if p is not None:
                            pe.wait_ge(bank.emptied.sem, bank.free(p, "gn"))
                            pe.wait_ge(gn[n].stats_ready.sem, gn[n].stats_ready.at(p, 1))
                            mm(bank.t[:, 0:8], w[group][:], gn[n].mine[:].rearrange("p a b -> p (a b)"), True, True
                               ).then_inc(bank.filled.sem, 1)
                    for n in range(UNITS):
                        p = pair_of(t, u, ATT + n + 2)
                        if p is not None:
                            values2(p, n)
                    p = pair_of(t, u, L2_RT)
                    if p is not None:
                        pe.wait_ge(bank_b.emptied.sem, bank_b.free(min(p + 3, PAIRS) if isinstance(p, int) else p + 3, "pw0"))
                        pe.wait_ge(bank_n.emptied.sem, bank_n.free(p, "rt"))
                        pe.wait_ge(rden_done.sem, rden_done.at(p, 1))
                        for j in range(4):
                            last = nc.tensor.transpose(bank_n.t[0:H2, j * HALF:(j + 1) * HALF], rden2[:, j],
                                                       eye[0:HALF, 0:HALF])
                        last.then_inc(bank_n.filled.sem, 1)
                    for i in range(2):
                        p = pair_of(t, u, L2_REP[i])
                        if p is not None:
                            pe.wait_ge(bank_n.emptied.sem, bank_n.free(p, f"rep{i}"))
                            for c in range(KC):
                                last = mm(bank_n.t[:, of_image(c)], w["heads"][:, c], rt2[:, of_image(i)], True, True)
                            last.then_inc(bank_n.filled.sem, 1)
                    for c in range(KC):
                        p = pair_of(t, u, L2_PROJ[c])
                        if p is not None:
                            pe.wait_ge(bank_n.emptied.sem, bank_n.free(p, f"proj{c}"))
                            product(bank_n.t[:, 0:N2], lambda k: w["p2"][:, k, of_chunk(c)], lambda k: a2[:, :, k]
                                    ).then_inc(bank_n.filled.sem, 1)
                    for j in range(4):
                        p = pair_of(t, u, L3_V[j])
                        if p is not None:
                            pe.wait_ge(bank_e.emptied.sem, bank_e.free(p, f"v{j}"))
                            pe.wait_ge(gn[3].low.sem, gn[3].low.at(p, KC))
                            split_product(bank_e.t[0:HALF, 0:CH + 2], lambda a, k: xs3[:, a, k, of_tile(j // 2, j % 2)],
                                          lambda b, k: ws["v3"][:, b, k]).then_inc(bank_e.filled.sem, 1)
                    for c in range(KC):
                        p = pair_of(t, u, L3_Q[c])
                        if p is not None:
                            pe.wait_ge(bank_e.emptied.sem, bank_e.free(p, f"q{c}"))
                            split_product(bank_e.t[:, 0:N2], lambda a, k: ws["q3"][:, a, k, of_chunk(c)],
                                          lambda b, k: xs3[:, b, k]).then_inc(bank_e.filled.sem, 1)
                    for i in range(2):
                        p = pair_of(t, u, L3_S[i])
                        if p is not None:
                            pe.wait_ge(bank_e.emptied.sem, bank_e.free(p, f"s{i}"))
                            for tc in range(2):
                                last = product(bank_e.t[0:HALF, of_image(tc)], lambda k: qt3[:, k, of_tile(i, tc)],
                                               lambda k: xn3[:, k, of_image(i)])
                            last.then_inc(bank_e.filled.sem, 1)
                        p = pair_of(t, u, L3_T[i])
                        if p is not None:
                            pe.wait_ge(bank_e.emptied.sem, bank_e.free(p, f"t{i}"))
                            pe.wait_ge(p3_done.sem, p3_done.at(p, 2 * (i + 1)))
                            for tc in range(2):
                                for sc in range(2):
                                    last = nc.tensor.transpose(bank_e.t[0:HALF, of_tile(sc, tc)],
                                                               e3[:, 2 * i + tc, sc * HALF:(sc + 1) * HALF],
                                                               eye[0:HALF, 0:HALF])
                            last.then_inc(bank_e.filled.sem, 1)
                        p = pair_of(t, u, L3_O[i])
                        if p is not None:
                            pe.wait_ge(bank_e.emptied.sem, bank_e.free(p, f"o{i}"))
                            for m in range(KC):
                                last = product(bank_e.t[:, of_image(m)], lambda k: v3t[:, 2 * i + k, of_chunk(m)],
                                               lambda k: pt3[:, i, k])
                            last.then_inc(bank_e.filled.sem, 1)
            run(pe, step)


def rows(x):
    return np.ascontiguousarray(np.moveaxis(x.reshape(KC, 128, *x.shape[1:]), 0, 1))


def laid_out(v):
    z = {}
    both = lambda a, b: np.concatenate([rows(a), rows(b)], axis=1)
    twice = lambda a: np.repeat(rows(a), 2, axis=1)
    z["x"] = np.ascontiguousarray(
        v["x"].reshape(PAIRS, 2, KC, 128, TOK).transpose(0, 3, 2, 1, 4).reshape(PAIRS, 128, KC * N2))
    for q in "gbmv":
        z["bn_" + q] = both(v["L0_conv_bn1_" + q], v["L0_conv_bn2_" + q])
    z["dw1"] = rows(v["L0_conv_w_qkv_dw"].reshape(CH, 9))
    at = np.linspace(0.0, SIDE - 1, R7, dtype=np.float32)[:6]
    z["frac"] = np.broadcast_to((at - np.floor(at)).astype(np.float32), (128, 6)).copy()
    by_head = (np.arange(D0)[None, :] * H0 + np.arange(H0)[:, None]).reshape(-1)
    q, k, u = np.split(v["L0_conv_w_qkv_pw"], 3)
    z["q0"], z["k0"], z["v0"] = (rows(m[by_head].T) for m in (q, k, u))
    z["dw2"] = rows(v["L0_conv_w_out_dw"].reshape(CH, 9)[by_head])
    z["o0"] = rows(v["L0_conv_w_out_pw"].T[by_head])
    z["mlp0"] = rows(v["L0_conv_w_mlp"].T)
    table = v["L0_conv_rel_table"]
    side = 2 * R7 - 1
    r, c = np.arange(TOK) // SIDE // 2, np.arange(TOK) % SIDE // 2
    kr, kc = np.arange(T7) // R7, np.arange(T7) % R7
    at = (r[:, None] - kr[None] + R7 - 1) * side + (c[:, None] - kc[None] + R7 - 1)
    z["bias0"] = table[at].reshape(2, HALF, T7, 2, 2).transpose(1, 4, 0, 3, 2).reshape(HALF, 2, 4, T7)
    for n, size in ((32, 32), (8, 8)):
        z[f"group{n}"] = np.kron(np.eye(128 // size), np.full((size, size), 1.0 / size)).astype(np.float32)
    z["gn1_w"], z["gn1_b"] = twice(v["L1_conv_gn_w"]), twice(v["L1_conv_gn_b"])
    q, k, u = np.split(v["L1_conv_qkv_w"], 3)
    qb, kb, ub = np.split(v["L1_conv_qkv_b"], 3)
    z["q1"], z["qb1"], z["k1"], z["v1"] = rows(q.T), rows(qb), rows(k.T), rows(u)
    z["kvb1"] = np.broadcast_to(kb, (HALF, CH))
    z["vb1_rep"] = np.broadcast_to(rows(ub)[:, :, None], (128, KC, HALF))
    z["p1"], z["pb1"] = rows(v["L1_conv_proj_w"].T), rows(v["L1_conv_proj_b"])
    z["gn2_w"], z["gn2_b"] = twice(v["L2_conv_norm_w"]), twice(v["L2_conv_norm_b"])
    q, k, u = v["L2_conv_qkv_w"].reshape(H2, 3, D2, CH).transpose(1, 0, 2, 3).reshape(3, CH, CH)
    qb, kb, ub = v["L2_conv_qkv_b"].reshape(H2, 3, D2).transpose(1, 0, 2).reshape(3, CH)
    z["q2"], z["k2"], z["v2"] = rows(q.T), rows(k.T), rows(u.T)
    z["qb2"], z["kb2"], z["vb2"] = rows(qb), rows(kb), rows(ub)
    z["p2"], z["pb2"] = rows(v["L2_conv_proj_w"].T), rows(v["L2_conv_proj_b"])
    z["heads"] = np.repeat(np.eye(H2), D2, axis=1).reshape(H2, KC, 128).astype(np.float32)
    z["eye"] = np.eye(128, dtype=np.float32)
    z["gn3_w"], z["gn3_b"] = twice(v["L3_conv_gamma"]), twice(v["L3_conv_beta"])
    z["q3"], z["k3"], z["v3"], z["o3"] = (rows(v["L3_conv_w" + m]) for m in "qkvo")
    z["o3"] = rows(v["L3_conv_wo"].T)
    z["qb3"], z["kb3"], z["vb3"], z["ob3"] = (rows(v["L3_conv_b" + m]) for m in "qkvo")
    z["qb3_rep"] = np.broadcast_to(rows(v["L3_conv_bq"])[:, :, None], (128, KC, HALF))
    return {name: np.ascontiguousarray(tile) for name, tile in z.items()}


def kernel(**inputs):
    import concourse.bacc as bacc
    from concourse.bass_utils import run_bass_kernel_spmd

    nc = bacc.Bacc("TRN2", target_bir_lowering=False, num_devices=1)
    arrays = {f"in_{k}": v for k, v in laid_out({k: np.asarray(v) for k, v in inputs.items()}).items()}
    a = {k[3:]: nc.dram_tensor(k, v.shape, mybir.dt.from_np(v.dtype), kind="ExternalInput").ap() for k, v in arrays.items()}
    a["out"] = nc.dram_tensor("out_pairs", (PAIRS, 128, KC * N2), F32, kind="ExternalOutput").ap()
    build(nc, a)
    r = run_bass_kernel_spmd(nc, [arrays], core_ids=[0])
    got = r.results[0]["out_pairs"].reshape(PAIRS, 128, KC, 2, TOK)
    return np.ascontiguousarray(got.transpose(0, 3, 2, 1, 4)).reshape(IMAGES, CH, SIDE, SIDE)
```
